# Optimizing a Trainium2 kernel written in Bass

```python
import numpy as np
import jax
import jax.numpy as jnp

def _softmax(x, axis=-1):
    return jax.nn.softmax(x, axis=axis)

def _gelu(x):
    return jax.nn.gelu(x, approximate=True)

def _silu(x):
    return jax.nn.silu(x)

def _sigmoid(x):
    return jax.nn.sigmoid(x)

def _layernorm(x, axis=-1, eps=1e-05):
    m = jnp.mean(x, axis=axis, keepdims=True)
    v = jnp.var(x, axis=axis, keepdims=True)
    return (x - m) / jnp.sqrt(v + eps)

def _scatter_add(tgt, idx, src, axis=0):
    return tgt.at[idx].add(src)

def _segment_sum(src, seg, n):
    return jax.ops.segment_sum(src, seg, n)
kernel_name = 'mk_macaron_d1_jaxref_r8_7745a9'

def setup_inputs(seed: int=0):
    np.random.seed(seed)
    _w = jnp.asarray

    def _L0_attn_setup():
        import jax, jax.numpy as jnp
        import numpy as np
        BASE_THETA = 0.5
        K_DOP = 0.2
        K_NOR = 0.15
        K_SERO = 0.1
        DIM = 128
        key = jax.random.key(seed)
        ks = jax.random.split(key, 9)
        scale = 1.0 / np.sqrt(DIM)
        x = jax.random.normal(ks[0], (2, 256, DIM), dtype=jnp.float32)
        Wq = jax.random.normal(ks[1], (DIM, DIM), dtype=jnp.float32) * scale
        bq = jnp.zeros((DIM,), dtype=jnp.float32)
        Wk = jax.random.normal(ks[2], (DIM, DIM), dtype=jnp.float32) * scale
        bk = jnp.zeros((DIM,), dtype=jnp.float32)
        Wv = jax.random.normal(ks[3], (DIM, DIM), dtype=jnp.float32) * scale
        bv = jnp.zeros((DIM,), dtype=jnp.float32)
        Wo = jax.random.normal(ks[4], (DIM, DIM), dtype=jnp.float32) * scale
        bo = jnp.zeros((DIM,), dtype=jnp.float32)
        return {'x': x, 'Wq': Wq, 'bq': bq, 'Wk': Wk, 'bk': bk, 'Wv': Wv, 'bv': bv, 'Wo': Wo, 'bo': bo}
    _L0_attn_in = _L0_attn_setup()

    def _L0_ffn_setup():
        import jax, jax.numpy as jnp
        import numpy as np
        DIM = 128
        DEPTH = 2
        HEADS = 8
        DIM_HEAD = 64
        WINDOW = 64
        INNER = HEADS * DIM_HEAD
        HID = int(DIM * 4 * 2 / 3)
        B, N = (2, 1024)
        QK_SCALE = 8.0

        def shift_token(t):
            t1, t2 = jnp.split(t, 2, axis=-1)
            t2 = jnp.pad(t2, ((0, 0), (1, 0), (0, 0)))[:, :-1]
            return jnp.concatenate([t1, t2], axis=-1)

        def l2norm(t):
            return t / jnp.clip(jnp.linalg.norm(t, axis=-1, keepdims=True), 1e-12)

        def rotate_half(x):
            x1, x2 = jnp.split(x, 2, axis=-1)
            return jnp.concatenate([-x2, x1], axis=-1)

        def rotary_xpos(q, k):
            n = q.shape[-2]
            half_idx = jnp.arange(0, DIM_HEAD, 2, dtype=jnp.float32)
            inv_freq = 1.0 / 10000.0 ** (half_idx / DIM_HEAD)
            t = jnp.arange(n, dtype=jnp.float32)
            freqs = t[:, None] * inv_freq[None, :]
            freqs = jnp.concatenate([freqs, freqs], axis=-1)
            base = (half_idx + 0.4 * DIM_HEAD) / (1.4 * DIM_HEAD)
            power = (t - n // 2) / float(WINDOW // 2)
            scale = base[None, :] ** power[:, None]
            scale = jnp.concatenate([scale, scale], axis=-1)
            cos, sin = (jnp.cos(freqs), jnp.sin(freqs))
            q = q * cos * scale + rotate_half(q) * sin * scale
            k = k * cos / scale + rotate_half(k) * sin / scale
            return (q, k)

        def local_attention(q, k, v):
            b, h, n, d = q.shape
            w = n // WINDOW
            bq = q.reshape(b, h, w, WINDOW, d) * QK_SCALE
            bk = k.reshape(b, h, w, WINDOW, d)
            bv = v.reshape(b, h, w, WINDOW, d)

            def look_around(t):
                p = jnp.pad(t, ((0, 0), (0, 0), (1, 0), (0, 0), (0, 0)))
                return jnp.concatenate([p[:, :, :w], p[:, :, 1:]], axis=3)
            bk, bv = (look_around(bk), look_around(bv))
            bt = jnp.arange(n).reshape(w, WINDOW)
            btp = jnp.pad(bt, ((1, 0), (0, 0)), constant_values=-1)
            btk = jnp.concatenate([btp[:w], btp[1:]], axis=1)
            sim = jnp.einsum('bhwid,bhwjd->bhwij', bq, bk)
            i = bt[:, :, None]
            j = btk[:, None, :]
            mask = (i < j) | (i > j + WINDOW) | (j == -1)
            sim = jnp.where(mask, -jnp.finfo(sim.dtype).max, sim)
            attn = jax.nn.softmax(sim, axis=-1)
            out = jnp.einsum('bhwij,bhwjd->bhwid', attn, bv)
            return out.reshape(b, h, n, d)

        def _layer(x, wqkv, qs, ksc, wo, lg, lb, w1, b1, w2, b2):
            b, n, _ = x.shape
            h = shift_token(x)
            qkv = h @ wqkv
            q, k, v = jnp.split(qkv, 3, axis=-1)
            to_heads = lambda t: t.reshape(b, n, HEADS, DIM_HEAD).transpose(0, 2, 1, 3)
            q, k, v = (to_heads(q), to_heads(k), to_heads(v))
            q = l2norm(q) * qs
            k = l2norm(k) * ksc
            q, k = rotary_xpos(q, k)
            o = local_attention(q, k, v)
            o = o.transpose(0, 2, 1, 3).reshape(b, n, INNER)
            x = x + o @ wo
            h = shift_token(x)
            mu = h.mean(-1, keepdims=True)
            var = h.var(-1, keepdims=True)
            h = (h - mu) / jnp.sqrt(var + 1e-05) * lg + lb
            h = h @ w1 + b1
            a, g = jnp.split(h, 2, axis=-1)
            h = a * jax.nn.gelu(g, approximate=False)
            x = x + h @ w2 + b2
            return x
        key = jax.random.key(seed)
        ks = jax.random.split(key, 6)
        return {'x': jax.random.normal(ks[0], (B, N, DIM), jnp.float32), 'wqkv': jax.random.normal(ks[1], (DEPTH, DIM, 3 * INNER), jnp.float32) * 0.02, 'q_scale': jnp.ones((DEPTH, DIM_HEAD), jnp.float32), 'k_scale': jnp.ones((DEPTH, DIM_HEAD), jnp.float32), 'wo': jax.random.normal(ks[2], (DEPTH, INNER, DIM), jnp.float32) * 0.02, 'ln_g': jnp.ones((DEPTH, DIM), jnp.float32), 'ln_b': jnp.zeros((DEPTH, DIM), jnp.float32), 'w1': jax.random.normal(ks[3], (DEPTH, DIM, 2 * HID), jnp.float32) * 0.02, 'b1': jnp.zeros((DEPTH, 2 * HID), jnp.float32), 'w2': jax.random.normal(ks[4], (DEPTH, HID, DIM), jnp.float32) * 0.02, 'b2': jnp.zeros((DEPTH, DIM), jnp.float32)}
    _L0_ffn_in = _L0_ffn_setup()
    _d = {'L0_attn_x': _L0_attn_in['x'], 'L0_attn_Wq': _L0_attn_in['Wq'], 'L0_attn_bq': _L0_attn_in['bq'], 'L0_attn_Wk': _L0_attn_in['Wk'], 'L0_attn_bk': _L0_attn_in['bk'], 'L0_attn_Wv': _L0_attn_in['Wv'], 'L0_attn_bv': _L0_attn_in['bv'], 'L0_attn_Wo': _L0_attn_in['Wo'], 'L0_attn_bo': _L0_attn_in['bo'], 'L0_ffn_wqkv': _L0_ffn_in['wqkv'], 'L0_ffn_q_scale': _L0_ffn_in['q_scale'], 'L0_ffn_k_scale': _L0_ffn_in['k_scale'], 'L0_ffn_wo': _L0_ffn_in['wo'], 'L0_ffn_ln_g': _L0_ffn_in['ln_g'], 'L0_ffn_ln_b': _L0_ffn_in['ln_b'], 'L0_ffn_w1': _L0_ffn_in['w1'], 'L0_ffn_b1': _L0_ffn_in['b1'], 'L0_ffn_w2': _L0_ffn_in['w2'], 'L0_ffn_b2': _L0_ffn_in['b2']}
    _x0 = _d['L0_attn_x']
    _d['L0_attn_x'] = jax.random.normal(jax.random.fold_in(jax.random.key(seed), 1), (8, 1024, 128), dtype=_x0.dtype)
    del _x0
    return _d

def reference(L0_attn_x, L0_attn_Wq, L0_attn_bq, L0_attn_Wk, L0_attn_bk, L0_attn_Wv, L0_attn_bv, L0_attn_Wo, L0_attn_bo, L0_ffn_wqkv, L0_ffn_q_scale, L0_ffn_k_scale, L0_ffn_wo, L0_ffn_ln_g, L0_ffn_ln_b, L0_ffn_w1, L0_ffn_b1, L0_ffn_w2, L0_ffn_b2):

    def _L0_attn_ref(x, Wq, bq, Wk, bk, Wv, bv, Wo, bo):
        import jax, jax.numpy as jnp
        import numpy as np
        BASE_THETA = 0.5
        K_DOP = 0.2
        K_NOR = 0.15
        K_SERO = 0.1
        DIM = 128
        q = jnp.einsum('bsd,ed->bse', x, Wq) + bq
        k = jnp.einsum('bsd,ed->bse', x, Wk) + bk
        v = jnp.einsum('bsd,ed->bse', x, Wv) + bv
        qk = jnp.einsum('bsd,btd->bst', q, k)
        theta = BASE_THETA + K_DOP * jax.nn.sigmoid(qk) + K_NOR * jnp.tanh(qk) + K_SERO * jax.nn.relu(qk)
        attn = jax.nn.softmax(theta, axis=-1)
        out = jnp.einsum('bst,btd->bsd', attn, v)
        return jnp.einsum('bsd,ed->bse', out, Wo) + bo

    def _L0_ffn_ref(x, wqkv, q_scale, k_scale, wo, ln_g, ln_b, w1, b1, w2, b2):
        import jax, jax.numpy as jnp
        import numpy as np
        DIM = 128
        DEPTH = 2
        HEADS = 8
        DIM_HEAD = 64
        WINDOW = 64
        INNER = HEADS * DIM_HEAD
        HID = int(DIM * 4 * 2 / 3)
        B, N = (2, 1024)
        QK_SCALE = 8.0

        def shift_token(t):
            t1, t2 = jnp.split(t, 2, axis=-1)
            t2 = jnp.pad(t2, ((0, 0), (1, 0), (0, 0)))[:, :-1]
            return jnp.concatenate([t1, t2], axis=-1)

        def l2norm(t):
            return t / jnp.clip(jnp.linalg.norm(t, axis=-1, keepdims=True), 1e-12)

        def rotate_half(x):
            x1, x2 = jnp.split(x, 2, axis=-1)
            return jnp.concatenate([-x2, x1], axis=-1)

        def rotary_xpos(q, k):
            n = q.shape[-2]
            half_idx = jnp.arange(0, DIM_HEAD, 2, dtype=jnp.float32)
            inv_freq = 1.0 / 10000.0 ** (half_idx / DIM_HEAD)
            t = jnp.arange(n, dtype=jnp.float32)
            freqs = t[:, None] * inv_freq[None, :]
            freqs = jnp.concatenate([freqs, freqs], axis=-1)
            base = (half_idx + 0.4 * DIM_HEAD) / (1.4 * DIM_HEAD)
            power = (t - n // 2) / float(WINDOW // 2)
            scale = base[None, :] ** power[:, None]
            scale = jnp.concatenate([scale, scale], axis=-1)
            cos, sin = (jnp.cos(freqs), jnp.sin(freqs))
            q = q * cos * scale + rotate_half(q) * sin * scale
            k = k * cos / scale + rotate_half(k) * sin / scale
            return (q, k)

        def local_attention(q, k, v):
            b, h, n, d = q.shape
            w = n // WINDOW
            bq = q.reshape(b, h, w, WINDOW, d) * QK_SCALE
            bk = k.reshape(b, h, w, WINDOW, d)
            bv = v.reshape(b, h, w, WINDOW, d)

            def look_around(t):
                p = jnp.pad(t, ((0, 0), (0, 0), (1, 0), (0, 0), (0, 0)))
                return jnp.concatenate([p[:, :, :w], p[:, :, 1:]], axis=3)
            bk, bv = (look_around(bk), look_around(bv))
            bt = jnp.arange(n).reshape(w, WINDOW)
            btp = jnp.pad(bt, ((1, 0), (0, 0)), constant_values=-1)
            btk = jnp.concatenate([btp[:w], btp[1:]], axis=1)
            sim = jnp.einsum('bhwid,bhwjd->bhwij', bq, bk)
            i = bt[:, :, None]
            j = btk[:, None, :]
            mask = (i < j) | (i > j + WINDOW) | (j == -1)
            sim = jnp.where(mask, -jnp.finfo(sim.dtype).max, sim)
            attn = jax.nn.softmax(sim, axis=-1)
            out = jnp.einsum('bhwij,bhwjd->bhwid', attn, bv)
            return out.reshape(b, h, n, d)

        def _layer(x, wqkv, qs, ksc, wo, lg, lb, w1, b1, w2, b2):
            b, n, _ = x.shape
            h = shift_token(x)
            qkv = h @ wqkv
            q, k, v = jnp.split(qkv, 3, axis=-1)
            to_heads = lambda t: t.reshape(b, n, HEADS, DIM_HEAD).transpose(0, 2, 1, 3)
            q, k, v = (to_heads(q), to_heads(k), to_heads(v))
            q = l2norm(q) * qs
            k = l2norm(k) * ksc
            q, k = rotary_xpos(q, k)
            o = local_attention(q, k, v)
            o = o.transpose(0, 2, 1, 3).reshape(b, n, INNER)
            x = x + o @ wo
            h = shift_token(x)
            mu = h.mean(-1, keepdims=True)
            var = h.var(-1, keepdims=True)
            h = (h - mu) / jnp.sqrt(var + 1e-05) * lg + lb
            h = h @ w1 + b1
            a, g = jnp.split(h, 2, axis=-1)
            h = a * jax.nn.gelu(g, approximate=False)
            x = x + h @ w2 + b2
            return x
        for l in range(DEPTH):
            x = _layer(x, wqkv[l], q_scale[l], k_scale[l], wo[l], ln_g[l], ln_b[l], w1[l], b1[l], w2[l], b2[l])
        return x
    x = L0_attn_x
    x = x + 0.5 * _L0_ffn_ref(_layernorm(x, axis=-1), L0_ffn_wqkv, L0_ffn_q_scale, L0_ffn_k_scale, L0_ffn_wo, L0_ffn_ln_g, L0_ffn_ln_b, L0_ffn_w1, L0_ffn_b1, L0_ffn_w2, L0_ffn_b2)
    x = x + _L0_attn_ref(_layernorm(x, axis=-1), L0_attn_Wq, L0_attn_bq, L0_attn_Wk, L0_attn_bk, L0_attn_Wv, L0_attn_bv, L0_attn_Wo, L0_attn_bo)
    x = x + 0.5 * _L0_ffn_ref(_layernorm(x, axis=-1), L0_ffn_wqkv, L0_ffn_q_scale, L0_ffn_k_scale, L0_ffn_wo, L0_ffn_ln_g, L0_ffn_ln_b, L0_ffn_w1, L0_ffn_b1, L0_ffn_w2, L0_ffn_b2)
    return x

_drawn_inputs = setup_inputs


def setup_inputs(seed=0):
    import zlib

    import numpy as np

    out = dict(_drawn_inputs(seed))
    spreads = {'L0_attn_bq': (0.0, 2.0),
     'L0_attn_bk': (0.0, 2.0),
     'L0_attn_bv': (0.0, 0.339),
     'L0_attn_bo': (0.0, 0.33),
     'L0_ffn_q_scale': (1.0, 0.6),
     'L0_ffn_k_scale': (1.0, 0.6),
     'L0_ffn_ln_g': (1.0, 0.6),
     'L0_ffn_ln_b': (0.0, 0.8),
     'L0_ffn_b1': (0.0, 0.8),
     'L0_ffn_b2': (0.0, 0.1)}
    factors = {'L0_ffn_wqkv': 3.281,
     'L0_ffn_wo': 3.283,
     'L0_ffn_w1': 5.334,
     'L0_ffn_w2': 5.244,
     'L0_attn_Wq': 2.806}
    for name, (base, spread) in spreads.items():
        noise = np.random.default_rng([zlib.crc32(name.encode()), seed]).standard_normal(out[name].shape)
        drawn = base * np.exp(spread * noise) if base else spread * noise
        out[name] = jnp.asarray(drawn.astype(out[name].dtype))
    for name, factor in factors.items():
        out[name] = (out[name] * factor).astype(out[name].dtype)
    return out
```

```python
from contextlib import ExitStack

import numpy as np

import concourse.bass as bass
from concourse import mybir

F32 = mybir.dt.float32
BF16 = mybir.dt.bfloat16
ACT = mybir.ActivationFunctionType
ALU = mybir.AluOpType
AX_X = mybir.AxisListType.X

P = 128
HEADS, DH, WIN = 8, 64, 64
INNER = HEADS * DH
HALF = P // 2
DEPTH = 2
HID = int(P * 4 * 2 / 3)
HID_CHUNKS = [(c, min(P, HID - c)) for c in range(0, HID, P)]
GROUP = 4
GCOLS = GROUP * P
QK_SCALE = 8.0
MASKED = -1e30
HD1 = DH + 1
BANK = 512
KT = WIN + P


def rotary_tables(n):
    half = np.arange(0, DH, 2, dtype=np.float32)
    inv_freq = (1.0 / (10000.0 ** (half / DH).astype(np.float64))).astype(np.float32)
    t = np.arange(n, dtype=np.float32)
    freqs = (t[:, None] * inv_freq[None, :]).astype(np.float64)
    base = ((half + 0.4 * DH) / (1.4 * DH)).astype(np.float32)
    power = (t - n // 2) / float(WIN // 2)
    scale = base[None, :].astype(np.float64) ** power[:, None].astype(np.float64)
    cos, sin = np.cos(freqs), np.sin(freqs)
    q, k = QK_SCALE * scale, 1.0 / scale
    pair = lambda a, b: np.concatenate([a, b], axis=-1)
    out = np.stack([pair(cos * q, cos * q), pair(cos * k, cos * k),
                    pair(-sin * q, sin * q), pair(-sin * k, sin * k)])
    return out.astype(np.float32)


def window_masks():
    i = np.arange(P)[:, None] % WIN
    j = np.arange(P)[None, :]
    open_ = (j >= i) & (j <= i + WIN)
    first = open_ & ((np.arange(P)[:, None] >= WIN) | (j >= WIN))
    return np.stack([np.tile(np.where(m, 0.0, MASKED), (1, 4)) for m in (first, open_)]).astype(np.float32)


class Tile:

    def __init__(self, seq_n, count, group, sequence, m):
        self.row, self.n, self.g, self.b, self.m = seq_n, count, group, sequence, m


def macaron(nc, x_in, wq_in, bq_in, wk_in, bk_in, wv_in, bv_in, wo_in, bo_in,
            wqkv_in, qs_in, ks_in, fwo_in, lng_in, lnb_in, w1_in, b1_in, w2_in, b2_in,
            rot_in, mask_in, id_in, out):
    B, N, D = x_in.shape
    MT = N // P
    NT = B * MT
    NG = NT // GROUP
    x_rows = x_in.rearrange("b (m p) d -> b p m d", p=P)
    out_rows = out.rearrange("b (m p) d -> b p m d", p=P)

    with ExitStack() as whole:
        def keep(name, shape, dt=F32):
            return whole.enter_context(nc.sbuf_tensor(name, shape, dt))

        X = keep("X", [P, NT, D])
        Y = keep("Y", [P, NT, D])
        ident = keep("ident", [P, P])
        neg_half = keep("neg_half", [P, 16])
        ones_row = keep("ones_row", [1, P])
        psum = whole.enter_context(nc.psum_tensor("psum", [P, 8 * BANK], F32))

        held = {}

        def sems(name):
            if name not in held:
                held[name] = whole.enter_context(nc.semaphore(name))
            return held[name]

        def bank(i, lo=0, hi=BANK, rows=slice(0, P)):
            return psum[rows, i * BANK + lo:i * BANK + hi]

        load_and_constants(nc, sems, X, ident, neg_half, ones_row, x_rows, id_in, B, MT)
        for call in range(2):
            layer_norm(nc, sems, f"pre{call}", X, Y, neg_half, B, MT)
            feed_forward(nc, sems, call, Y, ident, neg_half, ones_row, psum, bank, B, MT,
                         wqkv_in, qs_in, ks_in, fwo_in, lng_in, lnb_in, w1_in, b1_in, w2_in, b2_in,
                         rot_in, mask_in)
            add_half(nc, sems, f"half{call}", X, Y, B, MT, out_rows if call else None)
            if call == 0:
                layer_norm(nc, sems, "att", X, Y, neg_half, B, MT)
                attention(nc, sems, X, Y, ident, ones_row, bank, B, MT,
                          wq_in, bq_in, wk_in, bk_in, wv_in, bv_in, wo_in, bo_in)


def wait(engine, semaphore, value):
    if value is not None and not (isinstance(value, int) and value <= 0):
        engine.wait_ge(semaphore, value)


def load_and_constants(nc, sems, X, ident, neg_half, ones_row, x_rows, id_in, B, MT):
    with ExitStack() as ctx:
        loaded = sems("loaded")
        consts = sems("consts")
        block = ctx.enter_context(nc.Block())

        @block.sync
        def _(sp):
            for b in range(B):
                sp.dma_start(X[:, b * MT:(b + 1) * MT, :], x_rows[b]).then_inc(loaded, 16)
            sp.dma_start(ident[:], id_in).then_inc(loaded, 16)
            sp.wait_ge(loaded, 16 * (B + 1))

        @block.vector
        def _(dve):
            nc.vector.memset(neg_half[:], -0.5).then_inc(consts, 1)
            nc.vector.memset(ones_row[:], 1.0).then_inc(consts, 1)
            dve.wait_ge(consts, 2)


def layer_norm(nc, sems, name, src, dst, neg_half, B, MT):
    with ExitStack() as ctx:
        sem = lambda n: sems(f"{name}_{n}")
        sb = lambda n, s: ctx.enter_context(nc.sbuf_tensor(f"{name}_{n}", s, F32))
        stats = sb("stats", [P, 2, MT, 6])
        mean_var = sb("mean_var", [P, 2, MT, 2])
        rstd = sb("rstd", [P, 2, MT])
        stats_done, var_done, var_eps, rstd_done, normed = map(
            sem, ("stats_done", "var_done", "var_eps", "rstd_done", "normed"))
        block = ctx.enter_context(nc.Block())

        @block.gpsimd
        def _(pool):
            for b in range(B):
                pool.wait_ge(var_eps, b + 1)
                nc.gpsimd.tensor_tensor(rstd[:, b % 2, :], rstd[:, b % 2, :], neg_half[:, 0:MT],
                                        ALU.pow).then_inc(rstd_done, 1)

        @block.vector
        def _(dve):
            def statistics(b):
                if b >= 2:
                    dve.wait_ge(normed, MT * (b - 1))
                for m in range(MT):
                    nc.vector.bn_stats(stats[:, b % 2, m, :], src[:, b * MT + m, :]).then_inc(stats_done, 1)
                dve.wait_ge(stats_done, MT * (b + 1))
                for m in range(MT):
                    nc.vector.bn_aggr(mean_var[:, b % 2, m, :], stats[:, b % 2, m, :]).then_inc(var_done, 1)
                dve.wait_ge(var_done, MT * (b + 1))
                nc.vector.tensor_scalar_add(rstd[:, b % 2, :], mean_var[:, b % 2, :, 1], 1e-5).then_inc(var_eps, 1)

            def normalise(b):
                dve.wait_ge(rstd_done, b + 1)
                for m in range(MT):
                    nc.vector.tensor_scalar(dst[:, b * MT + m, :], src[:, b * MT + m, :],
                                            mean_var[:, b % 2, m, 0:1], rstd[:, b % 2, m:m + 1],
                                            ALU.subtract, ALU.mult).then_inc(normed, 1)

            statistics(0)
            for b in range(B):
                if b + 1 < B:
                    statistics(b + 1)
                normalise(b)
            dve.wait_ge(normed, MT * B)


def add_half(nc, sems, name, X, Y, B, MT, out_rows):
    with ExitStack() as ctx:
        added = sems(f"{name}_added")
        stored = sems(f"{name}_stored")
        block = ctx.enter_context(nc.Block())

        @block.vector
        def _(dve):
            for b in range(B):
                xs, ys = (t[:, b * MT:(b + 1) * MT, :].rearrange("p m d -> p (m d)") for t in (X, Y))
                nc.vector.scalar_tensor_tensor(out=xs, in0=ys, scalar=0.5, in1=xs, op0=ALU.mult,
                                               op1=ALU.add).then_inc(added, 1)
            dve.wait_ge(added, B)

        if out_rows is not None:
            @block.sync
            def _(sp):
                for b in range(B):
                    sp.wait_ge(added, b + 1)
                    sp.dma_start(out_rows[b], X[:, b * MT:(b + 1) * MT, :]).then_inc(stored, 16)
                sp.wait_ge(stored, 16 * B)


def feed_forward(nc, sems, call, Y, ident, neg_half, ones_row, psum, bank, B, MT,
                 wqkv_in, qs_in, ks_in, wo_in, lng_in, lnb_in, w1_in, b1_in, w2_in, b2_in,
                 rot_in, mask_in):
    NT = B * MT
    assert MT == 8 and GROUP == 4
    name = "ffn"
    with ExitStack() as ctx:
        sb = lambda n, s, dt=F32: ctx.enter_context(nc.sbuf_tensor(f"{name}{call}_{n}", s, dt))
        sem = lambda n: sems(f"{name}_{n}")

        wqkv = sb("wqkv", [P, 3 * INNER])
        wo = sb("wo", [P, INNER // P, P])
        w1 = sb("w1", [P, 2 * HID])
        w1g = sb("w1g", [P, 2 * HID])
        w2 = sb("w2", [P, len(HID_CHUNKS), P])
        b1 = sb("b1", [P, 2, len(HID_CHUNKS)])
        b1g = sb("b1g", [P, 2, len(HID_CHUNKS)])
        b2 = sb("b2", [1, P])
        lng = sb("lng", [P, 1])
        lnb = sb("lnb", [P, 1])
        qks = sb("qks", [P, 2, DH])
        rot = sb("rot", [P, 4, MT, DH])
        cos = sb("cos", [P, MT, 2, DH])
        sin = sb("sin", [P, MT, 2, DH])
        mask32 = sb("mask32", [P, 2, BANK])
        mask = sb("mask", [P, 2, BANK], BF16)
        zero_row = sb("zero_row", [1, HALF])
        ident16 = sb("ident16", [P, P], BF16)
        ystage = sb("ystage", [P, 4, P])
        hT = sb("hT", [P, MT * P + 1])
        sq = sb("sq", [P, 2 * INNER])
        ssq = sb("ssq", [P, 16])
        ssq_floor = sb("ssq_floor", [P, 16])
        rnorm = sb("rnorm", [P, 16])
        qkn = sb("qkn", [P, 2 * INNER])
        qk_cos = sb("qk_cos", [P, 2 * INNER])
        qk_sin = sb("qk_sin", [P, 2 * INNER])
        qkr = sb("qkr", [P, 2 * INNER])
        qT = sb("qT", [P, 2, 4, P])
        kT = sb("kT", [P, 2, 4, KT])
        v = sb("v", [P, 4, HEADS, HD1])
        vprev = sb("vprev", [P, 4, HEADS, HD1])
        neg_max = sb("neg_max", [P, HEADS])
        shifted = sb("shifted", [P, HEADS * P])
        probs = sb("probs", [P, HEADS * P])
        probsT = sb("probsT", [P, HEADS * P])
        rsum = sb("rsum", [P, HEADS])
        o = sb("o", [P, INNER])
        oT = sb("oT", [P, INNER])
        x1 = sb("x1", [P, MT, 3, HALF])
        stats = sb("stats", [P, GROUP, 6])
        half_even, mean, half_diff, half_diff_sq, spread, spread_eps = (
            sb(n, [P, GROUP]) for n in ("half_even", "mean", "half_diff", "half_diff_sq", "spread", "spread_eps"))
        var_eps = sb("var_eps", [P, GROUP])
        rstd = sb("rstd", [P, GROUP])
        z = sb("z", [P, GROUP, P])
        zT = sb("zT", [P, GCOLS])
        gate = sb("gate", [P, 2, GCOLS])
        hid = sb("hid", [P, len(HID_CHUNKS), GCOLS])

        (consts_in, consts_done, w_in, scales_in, w_ready, b1_psum, tables_ready, w1g_ready, b1_ready,
         staged_T, hT_ready, qk_psum, qkv_ready, sq_ready, v_ready, ssq_ready, floor_ready,
         rnorm_ready, qkn_ready, cos_ready, sin_ready, qkr_ready, qkT_psum, qkT_ready,
         scores_ready, max_ready, shifted_ready, probs_ready, probsT_psum, probsT_ready,
         pv_ready, rsum_ready, o_ready, oT_psum, oT_ready, attn_ready, x1_ready, 
         stats_ready, var_ready, eps_ready, rstd_ready, z_ready, zT_psum, zT_ready, ag_psum,
         gate_ready, hid_ready, mlp_ready, y_ready) = map(sem, """consts_in consts_done w_in scales_in
         w_ready b1_psum tables_ready w1g_ready b1_ready staged_T hT_ready qk_psum qkv_ready sq_ready
         v_ready ssq_ready floor_ready rnorm_ready qkn_ready cos_ready sin_ready qkr_ready
         qkT_psum qkT_ready scores_ready max_ready shifted_ready probs_ready probsT_psum probsT_ready
         pv_ready rsum_ready o_ready oT_psum oT_ready attn_ready x1_ready stats_ready
         var_ready eps_ready rstd_ready z_ready zT_psum zT_ready ag_psum gate_ready hid_ready
         mlp_ready y_ready""".split())

        W_DMAS = 9 + 4 * 0 + 2 * len(HID_CHUNKS)
        staged = [sem(f"staged{i}") for i in range(4)]
        vprev_ready = [sem(f"vprev_ready{i}") for i in range(4)]
        layer_over = sem("layer_over")
        x1_shifted = [sem(f"x1_shifted{i}") for i in range(2)]
        heads = lambda t: t.rearrange("p (h d) -> p h d", d=DH)
        FIRST, LAST = -3, NT + 3

        def layers(engine, start, slot, over=None):
            with engine.Fori(DEPTH * call, DEPTH * call + DEPTH) as l:
                start(l)

                def at(s, b, j):
                    def tile(d):
                        if b is None:
                            n = s + d
                            if not 0 <= n < NT:
                                return None
                            return Tile(n, l * NT + n, l * (NT // GROUP) + n // GROUP, l * B + n // MT, n % MT)
                        n = j + d
                        return Tile(b * MT + n, l * NT + b * MT + n,
                                    l * (NT // GROUP) + b * (MT // GROUP) + n // GROUP,
                                    l * B + b + n // MT, n % MT)
                    return tile

                for s in range(FIRST, MT):
                    slot(s % GROUP, at(s, None, None))
                with engine.Fori(1, B - 1) as b:
                    for j in range(MT):
                        slot(j % GROUP, at(None, b, j))
                for s in range(NT - MT, LAST):
                    slot(s % GROUP, at(s, None, None))
                engine.wait_ge(y_ready, (l + 1) * (NT // GROUP))
                if over is not None:
                    engine.sem_inc(over, 1)

        def before(t, k, times=1):
            local = t.row + 1 - k if isinstance(t.row, int) else 1
            return None if local <= 0 else times * (t.n + 1 - k)

        def group_before(t, k, times=1):
            local = t.row // GROUP + 1 - k if isinstance(t.row, int) else 1
            return None if local <= 0 else times * (t.g + 1 - k)

        block = ctx.enter_context(nc.Block())

        @block.sync
        def _(sp):
            sp.dma_start(rot[:], rot_in.rearrange("t (m p) d -> p t m d", p=P)).then_inc(consts_in, 16)
            sp.dma_start(mask32[:], mask_in.rearrange("t p c -> p t c")).then_inc(consts_in, 16)

            def start(l):
                row = lambda t: t[bass.ds(l - DEPTH * call, 1), :]
                sp.dma_start(qks[:, 0, :], row(qs_in).partition_broadcast(P)).then_inc(scales_in, 16)
                sp.dma_start(qks[:, 1, :], row(ks_in).partition_broadcast(P)).then_inc(scales_in, 16)
                sp.dma_start(wqkv[:], wqkv_in[bass.ds(l - DEPTH * call, 1)].rearrange("o d n -> d (o n)")).then_inc(w_in, 16)
                sp.dma_start(wo[:], wo_in[bass.ds(l - DEPTH * call, 1)].rearrange("o (c p) n -> p (o c) n", p=P)).then_inc(w_in, 16)
                sp.dma_start(w1[:], w1_in[bass.ds(l - DEPTH * call, 1)].rearrange("o d n -> d (o n)")).then_inc(w_in, 16)
                for c, (lo, size) in enumerate(HID_CHUNKS):
                    sp.dma_start(w2[0:size, c, :], w2_in[bass.ds(l - DEPTH * call, 1), lo:lo + size, :].rearrange(
                        "o p n -> p (o n)")).then_inc(w_in, 16)
                    for half in range(2):
                        sp.dma_start(b1[0:size, half, c:c + 1],
                                     b1_in[bass.ds(l - DEPTH * call, 1), half * HID + lo:half * HID + lo + size]
                                     .rearrange("o p -> p o")).then_inc(w_in, 16)
                sp.dma_start(b2[:], row(b2_in)).then_inc(w_in, 16)
                sp.dma_start(lng[:], row(lng_in).rearrange("o p -> p o")).then_inc(w_in, 16)
                sp.dma_start(lnb[:], row(lnb_in).rearrange("o p -> p o")).then_inc(w_in, 16)

            def slot(phase, tile):
                if t := tile(3):
                    row = t.row if isinstance(t.row, int) else sp.snap(t.row)
                    wait(sp, staged_T, before(t, 4))
                    sp.dma_start(ystage[:, t.m % 4, :], Y[:, bass.ds(row, 1), :]
                                 .rearrange("p o d -> p (o d)")).then_inc(staged[t.m % 4], 16)
                if t := tile(-1):
                    wait(sp, x1_ready, before(t, 0))
                    sp.dma_start(x1[1:P, t.m, 1, :], x1[0:P - 1, t.m, 2, :]).then_inc(x1_shifted[t.m // GROUP], 16)
                    if t.m:
                        sp.dma_start(x1[0:1, t.m, 1, :], x1[P - 1:P, t.m - 1, 2, :]).then_inc(x1_shifted[t.m // GROUP], 16)
                    else:
                        sp.dma_start(x1[0:1, 0, 1, :], zero_row[:]).then_inc(x1_shifted[t.m // GROUP], 16)
                if t := tile(2):
                    wait(sp, v_ready, before(t, 0))
                    sp.dma_start(vprev[WIN:P, t.m % 4], v[0:WIN, t.m % 4]).then_inc(vprev_ready[t.m % 4], 16)
                    lo = v[WIN:P, (t.m - 1) % 4] if t.m else v[0:WIN, 0]
                    sp.dma_start(vprev[0:WIN, t.m % 4], lo).then_inc(vprev_ready[t.m % 4], 16)

            sp.wait_ge(consts_done, 5 * call + 5)
            layers(sp, start, slot, layer_over)

        @block.gpsimd
        def _(pool):
            def slot(phase, tile):
                if phase == 1 and (t := tile(-5)):
                    pool.wait_ge(eps_ready, t.g + 1)
                    nc.gpsimd.tensor_tensor(rstd[:], var_eps[:], neg_half[:, 0:GROUP], ALU.pow).then_inc(rstd_ready, 1)
                if t := tile(2):
                    wait(pool, floor_ready, before(t, 0))
                    wait(pool, qkn_ready, before(t, 1))
                    nc.gpsimd.tensor_tensor(rnorm[:], ssq_floor[:], neg_half[:], ALU.pow).then_inc(rnorm_ready, 1)
                    wait(pool, qkn_ready, before(t, 0))
                    wait(pool, qkr_ready, before(t, 1))
                    x = qkn[:].rearrange("p (t h e d) -> p t h e d", t=2, h=HEADS, e=2)
                    y = qk_sin[:].rearrange("p (t h e d) -> p t h e d", t=2, h=HEADS, e=2)
                    s = sin[:, t.m].rearrange("p t (e d) -> p t e d", e=2)
                    for e in range(2):
                        nc.gpsimd.tensor_tensor(
                            y[:, :, :, e, :], x[:, :, :, 1 - e, :],
                            s[:, :, e, :].unsqueeze(2).to_broadcast([P, 2, HEADS, DH // 2]),
                            ALU.mult).then_inc(sin_ready, 1)

            def start(l):
                pool.wait_ge(tables_ready, 4 * l + 4)

            layers(pool, start, slot)

        @block.scalar
        def _(act):
            def start(l):
                act.wait_ge(b1_ready, 2 * l + 2)

            def slot(phase, tile):
                if phase == 2 and (t := tile(-6)):
                    act.wait_ge(zT_psum, t.g + 1)
                    wait(act, ag_psum, group_before(t, 1, 3))
                    nc.scalar.copy(zT[:], bank(5)).then_inc(zT_ready, 1)
                    for c, (lo, size) in enumerate(HID_CHUNKS):
                        act.wait_ge(ag_psum, 3 * t.g + c + 1)
                        wait(act, hid_ready, 3 * t.g + c - 1 if c >= 2 else group_before(t, 1, 3))
                        nc.scalar.activation(gate[0:size, c % 2, :], bank(6, rows=slice(0, size)),
                                             ACT.Gelu, bias=b1g[0:size, 1, c:c + 1]).then_inc(gate_ready, 1)
                if t := tile(-1):
                    if not (phase == 2 and tile(-6)):
                        out_of_heads(t)
                if t := tile(0):
                    for i in range(2):
                        cols = slice(i * BANK, (i + 1) * BANK)
                        act.wait_ge(shifted_ready, 2 * t.n + i + 1)
                        wait(act, probsT_psum, before(t, 1, 2))
                        nc.scalar.activation(probs[:, cols], shifted[:, cols], ACT.Exp).then_inc(probs_ready, 1)
                if t := tile(2):
                    wait(act, qk_psum, before(t, 0))
                    wait(act, ssq_ready, before(t, 1))
                    nc.scalar.activation(sq[:], psum[:, 0:2 * BANK], ACT.Square).then_inc(sq_ready, 1)
                    wait(act, qkv_ready, before(t, 0))
                    wait(act, pv_ready, before(t, 4))
                    if u := tile(-1):
                        act.wait_ge(vprev_ready[u.m % 4], 32 * (u.g + 1))
                    nc.scalar.copy(v[:, t.m % 4, :, 0:DH], heads(bank(2))).then_inc(v_ready, 1)
                if phase == 2 and tile(-6) and (t := tile(-1)):
                    out_of_heads(t)
                if t := tile(3):
                    wait(act, staged_T, before(t, 0))
                    wait(act, qkv_ready, before(t, MT - 1))
                    nc.scalar.copy(hT[0:HALF, t.m * P:(t.m + 1) * P], bank(7, 384, 512, slice(0, HALF))).then_inc(hT_ready, 1)
                    nc.scalar.copy(hT[HALF:P, t.m * P + 1:(t.m + 1) * P + 1],
                                   bank(7, 384, 512, slice(HALF, P))).then_inc(hT_ready, 1)
                if t := tile(0):
                    for i in range(2):
                        cols = slice(i * BANK, (i + 1) * BANK)
                        act.wait_ge(probsT_psum, 2 * t.n + i + 1)
                        wait(act, pv_ready, before(t, 1))
                        nc.scalar.copy(probsT[:, cols], bank(3 + i)).then_inc(probsT_ready, 1)
                if t := tile(1):
                    wait(act, qkT_psum, before(t, 0))
                    wait(act, scores_ready, before(t, 1))
                    nc.scalar.copy(qT[:, t.m % 2].rearrange("p c n -> p (c n)"), bank(5)).then_inc(qkT_ready, 1)
                    src = bank(6).rearrange("p (c n) -> p c n", n=P)
                    nc.scalar.copy(kT[:, t.m % 2, :, WIN:KT], src).then_inc(qkT_ready, 1)
                    nc.scalar.copy(kT[:, (t.m + 1) % 2, :, 0:WIN], src[:, :, WIN:P]).then_inc(qkT_ready, 1)

            def out_of_heads(t):
                wait(act, oT_psum, before(t, 0))
                wait(act, attn_ready, before(t, 1))
                nc.scalar.copy(oT[:], bank(5)).then_inc(oT_ready, 1)

            layers(act, start, slot)

        @block.vector
        def _(dve):
            nc.vector.memset(v[:, :, :, DH:HD1], 1.0).then_inc(consts_done, 1)
            nc.vector.memset(hT[HALF:P, 0:1], 0.0).then_inc(consts_done, 1)
            nc.vector.memset(zero_row[:], 0.0).then_inc(consts_done, 1)
            nc.vector.tensor_copy(ident16[:], ident[:]).then_inc(consts_done, 1)
            dve.wait_ge(consts_in, 32 * call + 32)
            nc.vector.tensor_copy(mask[:], mask32[:]).then_inc(consts_done, 1)

            def start(l):
                dve.wait_ge(scales_in, 32 * (l + 1))
                for t in range(2):
                    nc.vector.tensor_tensor(cos[:, :, t, :], rot[:, t], qks[:, t:t + 1, :].to_broadcast([P, MT, DH]),
                                            ALU.mult).then_inc(tables_ready, 1)
                for e in range(2):
                    for t in range(2):
                        lo, other = e * (DH // 2), (1 - e) * (DH // 2)
                        ins = nc.vector.tensor_tensor(
                            sin[:, :, t, lo:lo + DH // 2], rot[:, 2 + t, :, lo:lo + DH // 2],
                            qks[:, t:t + 1, other:other + DH // 2].to_broadcast([P, MT, DH // 2]), ALU.mult)
                        if e == 1:
                            ins.then_inc(tables_ready, 1)
                dve.wait_ge(w_in, 16 * 15 * (l + 1))
                nc.vector.tensor_scalar(w1g[:], w1[:], lng[:, 0:1], None, ALU.mult).then_inc(w1g_ready, 1)
                dve.wait_ge(b1_psum, l + 1)
                pb = bank(7, 0, 6).rearrange("p (h c) -> p h c", h=2)
                nc.vector.tensor_tensor(b1g[:, :, 0:2], b1[:, :, 0:2], pb[:, :, 0:2], ALU.add).then_inc(b1_ready, 1)
                last = HID_CHUNKS[-1][1]
                nc.vector.tensor_tensor(b1g[0:last, :, 2:3], b1[0:last, :, 2:3], pb[0:last, :, 2:3],
                                        ALU.add).then_inc(b1_ready, 1)

            def slot(phase, tile):
                if t := tile(0):
                    for i in range(2):
                        cols = slice(i * BANK, (i + 1) * BANK)
                        s = bank(3 + i).rearrange("p (h k) -> p h k", k=P)
                        wait(dve, scores_ready, before(t, 0))
                        wait(dve, shifted_ready, 2 * t.n + i if i else before(t, 1, 2))
                        nc.vector.tensor_reduce(neg_max[:, 4 * i:4 * i + 4], s, AX_X, ALU.max,
                                                negate=True).then_inc(max_ready, 1)
                        dve.wait_ge(max_ready, 2 * t.n + i + 1)
                        wait(dve, probs_ready, before(t, 1, 2))
                        nc.vector.tensor_tensor(
                            shifted[:, cols].rearrange("p (h k) -> p h k", k=P), s,
                            neg_max[:, 4 * i:4 * i + 4].unsqueeze(2).to_broadcast([P, 4, P]),
                            ALU.add).then_inc(shifted_ready, 1)
                if phase == 1 and (t := tile(-5)):
                    m0 = t.m
                    dve.wait_ge(x1_shifted[t.m // GROUP], 32 * GROUP * (t.b + 1))
                    h = lambda k: x1[:, m0 + k, 0:2, :].rearrange("p a d -> p (a d)")
                    for k in range(GROUP):
                        nc.vector.bn_stats(stats[:, k, :], h(k)).then_inc(stats_ready, 1)
                    dve.wait_ge(stats_ready, GROUP * (t.g + 1))
                    me, se, mo, so = (stats[:, :, i] for i in (1, 2, 4, 5))
                    nc.vector.tensor_scalar(half_even[:], me, 0.5, None, ALU.mult).then_inc(var_ready, 1)
                    nc.vector.tensor_tensor(spread[:], se, so, ALU.add).then_inc(var_ready, 1)
                    dve.wait_ge(var_ready, 6 * t.g + 2)
                    nc.vector.scalar_tensor_tensor(out=mean[:], in0=mo, scalar=0.5, in1=half_even[:],
                                                   op0=ALU.mult, op1=ALU.add).then_inc(var_ready, 1)
                    nc.vector.scalar_tensor_tensor(out=half_diff[:], in0=mo, scalar=-0.5, in1=half_even[:],
                                                   op0=ALU.mult, op1=ALU.add).then_inc(var_ready, 1)
                    nc.vector.tensor_scalar(spread_eps[:], spread[:], 1.0 / P, 1e-5, ALU.mult, ALU.add).then_inc(var_ready, 1)
                    dve.wait_ge(var_ready, 6 * t.g + 5)
                    nc.vector.tensor_tensor(half_diff_sq[:], half_diff[:], half_diff[:], ALU.mult).then_inc(var_ready, 1)
                    dve.wait_ge(var_ready, 6 * t.g + 6)
                    nc.vector.tensor_tensor(var_eps[:], half_diff_sq[:], spread_eps[:], ALU.add).then_inc(eps_ready, 1)
                    wait(dve, zT_psum, group_before(t, 1))
                    dve.wait_ge(rstd_ready, t.g + 1)
                    for k in range(GROUP):
                        nc.vector.tensor_scalar(z[:, k, :], h(k), mean[:, k:k + 1], rstd[:, k:k + 1],
                                                ALU.subtract, ALU.mult).then_inc(z_ready, 1)
                if phase == 2 and (t := tile(-6)):
                    for c, (lo, size) in enumerate(HID_CHUNKS):
                        dve.wait_ge(gate_ready, 3 * t.g + c + 1)
                        wait(dve, mlp_ready, group_before(t, 1))
                        nc.vector.scalar_tensor_tensor(
                            out=hid[0:size, c, :], in0=bank(5, rows=slice(0, size)),
                            scalar=b1g[0:size, 0, c:c + 1], in1=gate[0:size, c % 2, :],
                            op0=ALU.add, op1=ALU.mult).then_inc(hid_ready, 1)
                if t := tile(1):
                    wait(dve, qkn_ready, before(t, 0))
                    wait(dve, qkr_ready, before(t, 1))
                    nc.vector.tensor_tensor(
                        qk_cos[:].rearrange("p (t h d) -> p t h d", t=2, d=DH),
                        qkn[:].rearrange("p (t h d) -> p t h d", t=2, d=DH),
                        cos[:, t.m].unsqueeze(2).to_broadcast([P, 2, HEADS, DH]),
                        ALU.mult).then_inc(cos_ready, 1)
                if t := tile(1):
                    wait(dve, sin_ready, before(t, 0, 2))
                    wait(dve, cos_ready, before(t, 0))
                    wait(dve, qkT_psum, before(t, 1))
                    nc.vector.tensor_tensor(qkr[:], qk_cos[:], qk_sin[:], ALU.add).then_inc(qkr_ready, 1)
                if phase == 2 and (t := tile(-6)):
                    dve.wait_ge(mlp_ready, t.g + 1)
                    nc.vector.tensor_tensor(
                        Y[:, bass.ds(t.row, GROUP), :].rearrange("p m (a d) -> p m a d", a=2),
                        bank(5).rearrange("p (m a d) -> p m a d", m=GROUP, a=2),
                        x1[:, t.m:t.m + GROUP, 0:3:2, :], ALU.add).then_inc(y_ready, 1)
                if t := tile(-1):
                    wait(dve, attn_ready, before(t, 0))
                    if not (isinstance(t.row, int) and t.row < MT):
                        dve.wait_ge(y_ready, t.g - 1)
                    nc.vector.tensor_tensor(
                        x1[:, t.m, 0:3:2, :], bank(6, 0, P).rearrange("p (a d) -> p a d", a=2),
                        Y[:, bass.ds(t.row, 1), :].rearrange("p o (a d) -> p (o a) d", a=2),
                        ALU.add).then_inc(x1_ready, 1)
                if t := tile(2):
                    wait(dve, sq_ready, before(t, 0))
                    nc.vector.tensor_reduce(ssq[:], sq[:].rearrange("p (h d) -> p h d", d=DH), AX_X,
                                            ALU.add).then_inc(ssq_ready, 1)
                    wait(dve, ssq_ready, before(t, 0))
                    wait(dve, rnorm_ready, before(t, 1))
                    nc.vector.tensor_scalar_max(ssq_floor[:], ssq[:], 1e-24).then_inc(floor_ready, 1)
                if t := tile(0):
                    wait(dve, pv_ready, before(t, 0))
                    wait(dve, o_ready, before(t, 1, 2))
                    for i, bk in enumerate((7, 2)):
                        pv = bank(bk, 0, 4 * HD1).rearrange("p (h d) -> p h d", d=HD1)
                        nc.vector.reciprocal(rsum[:, 4 * i:4 * i + 4], pv[:, :, DH]).then_inc(rsum_ready, 1)
                    dve.wait_ge(rsum_ready, 2 * t.n + 2)
                    wait(dve, oT_psum, before(t, 1))
                    for i, bk in enumerate((7, 2)):
                        pv = bank(bk, 0, 4 * HD1).rearrange("p (h d) -> p h d", d=HD1)
                        nc.vector.tensor_tensor(
                            heads(o[:])[:, 4 * i:4 * i + 4, :], pv[:, :, 0:DH],
                            rsum[:, 4 * i:4 * i + 4].unsqueeze(2).to_broadcast([P, 4, DH]),
                            ALU.mult).then_inc(o_ready, 1)
                if t := tile(2):
                    wait(dve, rnorm_ready, before(t, 0))
                    wait(dve, sin_ready, before(t, 1, 2))
                    wait(dve, cos_ready, before(t, 1))
                    nc.vector.tensor_tensor(heads(qkn[:]), heads(psum[:, 0:2 * BANK]),
                                            rnorm[:].unsqueeze(2).to_broadcast([P, 16, DH]),
                                            ALU.mult).then_inc(qkn_ready, 1)

            layers(dve, start, slot)

        @block.tensor
        def _(pe):
            def start(l):
                pe.wait_ge(w_in, 16 * 15 * (l + 1))
                for half in range(2):
                    for c, (lo, size) in enumerate(HID_CHUNKS):
                        col = half * 3 + c
                        last = nc.tensor.matmul(bank(7, col, col + 1, slice(0, size)),
                                                w1[:, half * HID + lo:half * HID + lo + size], lnb[:, 0:1],
                                                start=True, stop=True)
                last.then_inc(b1_psum, 1)
                pe.wait_ge(b1_ready, 2 * l + 2)
                pe.wait_ge(w1g_ready, l + 1)
                pe.wait_ge(consts_done, 5 * call + 5)

            def mlp_transpose(t, tile):
                pe.wait_ge(z_ready, GROUP * (t.g + 1))
                if u := tile(0):
                    wait(pe, qkT_ready, before(u, 0, 3))
                if u := tile(-2):
                    wait(pe, x1_ready, before(u, 0))
                for k in range(GROUP):
                    last = nc.tensor.transpose(bank(5, k * P, (k + 1) * P), z[:, k, :], ident[:])
                last.then_inc(zT_psum, 1)

            def mlp_first(t, c):
                lo, size = HID_CHUNKS[c]
                if c == 0:
                    pe.wait_ge(zT_ready, t.g + 1)
                else:
                    pe.wait_ge(hid_ready, 3 * t.g + c)
                for half in range(2):
                    last = nc.tensor.matmul(bank(5 + half, rows=slice(0, size)),
                                            w1g[:, half * HID + lo:half * HID + lo + size], zT[:],
                                            start=True, stop=True)
                last.then_inc(ag_psum, 1)

            def mlp_second(t):
                pe.wait_ge(hid_ready, 3 * t.g + 3)
                for k in range(GROUP):
                    o_ = bank(5, k * P, (k + 1) * P)
                    nc.tensor.matmul(o_, ones_row[:], b2[:], start=True, stop=False)
                    for c, (lo, size) in enumerate(HID_CHUNKS):
                        last = nc.tensor.matmul(o_, hid[0:size, c, k * P:(k + 1) * P], w2[0:size, c, :],
                                                start=False, stop=(c == len(HID_CHUNKS) - 1))
                last.then_inc(mlp_ready, 1)

            def scores(t):
                wait(pe, qkT_ready, before(t, 0, 3))
                wait(pe, probsT_ready, before(t, 1, 2))
                for i in range(2):
                    nc.tensor.matmul(bank(3 + i), ident16[:], mask[:, 1 if t.m else 0, :],
                                     start=True, stop=False, skip_group_check=True)
                lo = 0 if t.m else WIN
                for hh in range(4):
                    for i in range(2):
                        rows = slice(DH * i, DH * i + DH)
                        q = qT[rows, t.m % 2, hh, :]
                        k = kT[rows, t.m % 2, hh, :]
                        nc.tensor.matmul(bank(3 + i, hh * P + lo, (hh + 1) * P, slice(0, WIN)), q[:, 0:WIN],
                                         k[:, lo:P], start=False, stop=True, skip_group_check=True)
                        last = nc.tensor.matmul(bank(3 + i, hh * P, (hh + 1) * P, slice(WIN, P)), q[:, WIN:P],
                                                k[:, WIN:KT], start=False, stop=True, skip_group_check=True)
                last.then_inc(scores_ready, 1)

            def heads_transpose(t):
                wait(pe, o_ready, before(t, 0, 2))
                for c in range(INNER // P):
                    last = nc.tensor.transpose(bank(5, c * P, (c + 1) * P), o[:, c * P:(c + 1) * P], ident[:])
                last.then_inc(oT_psum, 1)

            def project_qk(t):
                wait(pe, hT_ready, before(t, 0, 2))
                wait(pe, qkn_ready, before(t, 1))
                for i in range(2):
                    last = nc.tensor.matmul(bank(i), hT[:, t.m * P:(t.m + 1) * P],
                                            wqkv[:, i * INNER:(i + 1) * INNER], start=True, stop=True)
                last.then_inc(qk_psum, 1)

            def project_v(t, u):
                wait(pe, v_ready, before(t, 1))
                if u:
                    wait(pe, o_ready, before(u, 0, 2))
                nc.tensor.matmul(bank(2), hT[:, t.m * P:(t.m + 1) * P], wqkv[:, 2 * INNER:3 * INNER],
                                 start=True, stop=True).then_inc(qkv_ready, 1)

            def project_out(t):
                wait(pe, oT_ready, before(t, 0))
                for c in range(INNER // P):
                    last = nc.tensor.matmul(bank(6, 0, P), oT[:, c * P:(c + 1) * P], wo[:, c, :],
                                            start=(c == 0), stop=(c == INNER // P - 1))
                last.then_inc(attn_ready, 1)

            def tokens_transpose(t):
                pe.wait_ge(staged[t.m % 4], 16 * (t.g + 1))
                wait(pe, hT_ready, before(t, 1, 2))
                nc.tensor.transpose(bank(7, 384, 512), ystage[:, t.m % 4, :], ident[:]).then_inc(staged_T, 1)

            def weights_transpose(t):
                for i in range(2):
                    pe.wait_ge(probs_ready, 2 * t.n + i + 1)
                    for c in range(4 * i, 4 * i + 4):
                        last = nc.tensor.transpose(bank(3 + i, (c % 4) * P, (c % 4 + 1) * P),
                                                   probs[:, c * P:(c + 1) * P], ident[:])
                    last.then_inc(probsT_psum, 1)

            def rotated_transpose(t, u):
                wait(pe, qkr_ready, before(t, 0))
                if u:
                    wait(pe, x1_ready, before(u, 0))
                else:
                    wait(pe, qkT_ready, before(t, 1, 3))
                for c in range(8):
                    last = nc.tensor.transpose(bank(5 + c // 4, (c % 4) * P, (c % 4 + 1) * P),
                                               qkr[:, c * P:(c + 1) * P], ident[:])
                last.then_inc(qkT_psum, 1)

            def weigh_values(t):
                pe.wait_ge(vprev_ready[t.m % 4], 32 * (t.g + 1))
                wait(pe, o_ready, before(t, 1, 2))
                pe.wait_ge(probsT_ready, 2 * t.n + 2)
                for h in range(HEADS):
                    at_h = (h % 2) * BANK + (h // 2) * P
                    col = (h % 4) * HD1
                    lo = 0 if t.m else WIN
                    bk = (7, 2)[h // 4]
                    nc.tensor.matmul(bank(bk, col, col + HD1, slice(WIN, P)),
                                     probsT[:, at_h + WIN:at_h + P], v[:, t.m % 4, h, :],
                                     start=True, stop=True)
                    last = nc.tensor.matmul(bank(bk, col, col + HD1, slice(0, WIN)),
                                            probsT[lo:P, at_h:at_h + WIN], vprev[lo:P, t.m % 4, h, :],
                                            start=True, stop=True)
                last.then_inc(pv_ready, 1)

            def slot(phase, tile):
                mlp = tile(-6) if phase == 2 else None
                done, now, soon, next_, last_ = tile(-1), tile(0), tile(1), tile(2), tile(3)
                if mlp:
                    mlp_transpose(mlp, tile)
                if now:
                    scores(now)
                if mlp:
                    mlp_first(mlp, 0)
                elif done:
                    heads_transpose(done)
                if next_:
                    project_qk(next_)
                if mlp:
                    mlp_first(mlp, 1)
                if next_:
                    project_v(next_, done)
                if last_:
                    tokens_transpose(last_)
                if mlp:
                    mlp_first(mlp, 2)
                    mlp_second(mlp)
                    if done:
                        pe.wait_ge(y_ready, mlp.g + 1)
                        heads_transpose(done)
                if done:
                    project_out(done)
                if now:
                    weights_transpose(now)
                if soon:
                    rotated_transpose(soon, done)
                if now:
                    if next_:
                        pe.wait_ge(v_ready, next_.n + 1)
                    weigh_values(now)

            layers(pe, start, slot)


def attention(nc, sems, X, Y, ident, ones_row, bank, B, MT, wq_in, bq_in, wk_in, bk_in, wv_in, bv_in,
              wo_in, bo_in):
    N = MT * P
    with ExitStack() as ctx:
        sb = lambda n, s, dt=F32: ctx.enter_context(nc.sbuf_tensor(f"att_{n}", s, dt))
        sem = lambda n: sems(f"att_{n}")
        ys_in = [sem(f"ys_in{i}") for i in range(2)]
        w = sb("w", [P, 4, P])
        bias = sb("bias", [P, 3])
        bo = sb("bo", [1, P])
        bo_all = sb("bo_all", [P, P])
        ys = sb("ys", [P, 2, MT, P])
        xT = sb("xT", [P, N])
        qkvT = sb("qkvT", [P, 3, N])
        vo = sb("vo", [P, MT, P + 1])
        th_half = sb("th_half", [P, 2, N])
        th_full = sb("th_full", [P, 2, N])
        mix = sb("mix", [P, N])
        theta = sb("theta", [P, 2, N])
        top = sb("top", [P, 2])
        bias_top = sb("bias_top", [P, 2])
        probs = sb("probs", [P, 2, N])
        probsT = sb("probsT", [P, 2, N])
        rsum = sb("rsum", [P, 2])
        o = sb("o", [P, 2, P])
        (w_in, bo_psum, bo_ready, xT_psum, xT_ready, proj_psum, proj_ready, vo_psum, vo_ready,
         ones_done, scores_ready, half_ready, full_ready, mix_ready, theta_ready, top_ready, bias_ready,
         probs_ready, pT_psum, pT_ready, out_psum, rsum_ready, o_ready, obo_ready, x_ready) = map(
            sem, """w_in bo_psum bo_ready xT_psum xT_ready proj_psum proj_ready vo_psum vo_ready
            ones_done scores_ready half_ready full_ready mix_ready theta_ready top_ready bias_ready
            probs_ready pT_psum pT_ready out_psum rsum_ready o_ready obo_ready x_ready""".split())
        block = ctx.enter_context(nc.Block())

        def pairs(engine):
            yield 0
            with engine.Fori(1, B // 2) as b2:
                yield b2

        @block.sync
        def _(sp):
            for i, t in enumerate((wq_in, wk_in, wv_in, wo_in)):
                sp.dma_start(w[:, i, :], t).then_inc(w_in, 16)
            for i, t in enumerate((bq_in, bk_in, bv_in)):
                sp.dma_start(bias[:, i:i + 1], t.rearrange("(p o) -> p o", o=1)).then_inc(w_in, 16)
            sp.dma_start(bo[:], bo_in.rearrange("(o p) -> o p", o=1)).then_inc(w_in, 16)
            for b in range(2):
                sp.dma_start(ys[:, b], Y[:, b * MT:(b + 1) * MT, :]).then_inc(ys_in[b], 16)
            with sp.Fori(0, B // 2 - 1) as b2:
                for b in range(2):
                    row = sp.snap((b2 * 2 + b + 2) * MT)
                    wait(sp, xT_psum, 4 * b2 + 2 * b + 2)
                    sp.dma_start(ys[:, b], Y[:, bass.ds(row, MT), :]).then_inc(ys_in[b], 16)

        @block.tensor
        def _(pe):
            wait(pe, w_in, 16 * 8)
            nc.tensor.matmul(bank(7, 0, P), ones_row[:], bo[:], start=True, stop=True).then_inc(bo_psum, 1)
            wait(pe, bo_ready, 1)
            wait(pe, ones_done, 1)
            for b2 in pairs(pe):
                for par in range(2):
                    n = b2 * 2 + par
                    wait(pe, ys_in[par], 16 * (b2 + 1))
                    for i in range(2):
                        wait(pe, x_ready, 8 * n)
                        for m in range(4 * i, 4 * i + 4):
                            last = nc.tensor.transpose(bank(i, (m % 4) * P, (m % 4 + 1) * P), ys[:, par, m, :], ident[:])
                        last.then_inc(xT_psum, 1)
                    wait(pe, xT_ready, 2 * n + 2)
                    for i in range(3):
                        for half in range(2):
                            bk = (2 * i + half) % 6
                            last = nc.tensor.matmul(bank(bk), w[:, i, :], xT[:, half * BANK:(half + 1) * BANK],
                                                    start=True, stop=True)
                            last.then_inc(proj_psum, 1)
                    wait(pe, proj_ready, 6 * n + 6)
                    for i in range(2):
                        for m in range(4 * i, 4 * i + 4):
                            last = nc.tensor.matmul(bank(4 + i, (m % 4) * P, (m % 4 + 1) * P),
                                                    qkvT[:, 2, m * P:(m + 1) * P], w[:, 3, :], start=True, stop=True)
                        last.then_inc(vo_psum, 1)
                    wait(pe, vo_ready, 2 * n + 2)

                    def scores(m):
                        k = n * MT + m
                        wait(pe, theta_ready, k - 1)
                        wait(pe, full_ready, k - 1)
                        for half in range(2):
                            last = nc.tensor.matmul(bank(2 * (m % 2) + half), qkvT[:, 0, m * P:(m + 1) * P],
                                                    qkvT[:, 1, half * BANK:(half + 1) * BANK], start=True, stop=True)
                        last.then_inc(scores_ready, 1)

                    def weigh(m):
                        k = n * MT + m
                        wait(pe, probs_ready, k + 1)
                        for i in range(2):
                            wait(pe, pT_ready, 2 * k)
                            for c in range(4 * i, 4 * i + 4):
                                last = nc.tensor.transpose(bank(4 + i, (c % 4) * P, (c % 4 + 1) * P),
                                                           probs[:, m % 2, c * P:(c + 1) * P], ident[:])
                            last.then_inc(pT_psum, 1)

                    def product(m):
                        k = n * MT + m
                        wait(pe, pT_ready, 2 * k + 2)
                        wait(pe, o_ready, k - 1)
                        for c in range(MT):
                            last = nc.tensor.matmul(bank(6 + m % 2, 0, P + 1), probsT[:, m % 2, c * P:(c + 1) * P],
                                                    vo[:, c, :], start=(c == 0), stop=(c == MT - 1))
                        last.then_inc(out_psum, 1)

                    scores(0)
                    scores(1)
                    for m in range(MT):
                        weigh(m)
                        if m >= 1:
                            product(m - 1)
                        if m + 2 < MT:
                            scores(m + 2)
                    product(MT - 1)

        @block.scalar
        def _(act):
            for b2 in pairs(act):
                for par in range(2):
                    n = b2 * 2 + par
                    for i in range(2):
                        wait(act, xT_psum, 2 * n + i + 1)
                        wait(act, proj_psum, 6 * n)
                        nc.scalar.copy(xT[:, i * BANK:(i + 1) * BANK], bank(i)).then_inc(xT_ready, 1)
                    for m in range(MT + 1):
                        if m < MT:
                            k = n * MT + m
                            s = wide(bank, 2 * (m % 2))
                            wait(act, scores_ready, k + 1)
                            wait(act, mix_ready, k - 1)
                            nc.scalar.activation(th_half[:, m % 2, :], s, ACT.Tanh, scale=0.5).then_inc(half_ready, 1)
                            nc.scalar.activation(th_full[:, m % 2, :], s, ACT.Tanh).then_inc(full_ready, 1)
                        if m >= 1:
                            k = n * MT + m - 1
                            q = (m - 1) % 2
                            wait(act, bias_ready, k + 1)
                            wait(act, pT_psum, 2 * (k - 1))
                            nc.scalar.activation(probs[:, q, :], theta[:, q, :], ACT.Exp, bias=bias_top[:, q:q + 1],
                                                 scale=0.1).then_inc(probs_ready, 1)
                            wait(act, out_psum, k - 1)
                            for i in range(2):
                                wait(act, pT_psum, 2 * k + i + 1)
                                nc.scalar.copy(probsT[:, q, i * BANK:(i + 1) * BANK], bank(4 + i)).then_inc(pT_ready, 1)

        @block.vector
        def _(dve):
            nc.vector.memset(vo[:, :, P:P + 1], 1.0).then_inc(ones_done, 1)
            wait(dve, bo_psum, 1)
            nc.vector.tensor_copy(bo_all[:], bank(7, 0, P)).then_inc(bo_ready, 1)
            for b2 in pairs(dve):
                for par in range(2):
                    n = b2 * 2 + par
                    for i in range(3):
                        for half in range(2):
                            wait(dve, proj_psum, 6 * n + 2 * i + half + 1)
                            nc.vector.tensor_scalar(qkvT[:, i, half * BANK:(half + 1) * BANK], bank((2 * i + half) % 6),
                                                    bias[:, i:i + 1], None, ALU.add).then_inc(proj_ready, 1)
                    for i in range(2):
                        wait(dve, vo_psum, 2 * n + i + 1)
                        nc.vector.tensor_copy(vo[:, 4 * i:4 * i + 4, 0:P],
                                              bank(4 + i).rearrange("p (m d) -> p m d", d=P)).then_inc(vo_ready, 1)

                    def finish(m):
                        k = n * MT + m
                        q = m % 2
                        acc = bank(6 + q, 0, P + 1)
                        wait(dve, out_psum, k + 1)
                        nc.vector.reciprocal(rsum[:, q:q + 1], acc[:, P:P + 1]).then_inc(rsum_ready, 1)
                        wait(dve, rsum_ready, k + 1)
                        nc.vector.scalar_tensor_tensor(out=o[:, q, :], in0=acc[:, 0:P], scalar=rsum[:, q:q + 1],
                                                       in1=bo_all[:], op0=ALU.mult, op1=ALU.add).then_inc(o_ready, 1)
                        wait(dve, o_ready, k + 1)
                        xs = X[:, bass.ds(k, 1), :].rearrange("p o d -> p (o d)")
                        nc.vector.tensor_tensor(xs, xs, o[:, q, :], ALU.add).then_inc(x_ready, 1)

                    for m in range(MT):
                        k = n * MT + m
                        q = m % 2
                        wait(dve, full_ready, k + 1)
                        wait(dve, theta_ready, k)
                        nc.vector.scalar_tensor_tensor(out=mix[:], in0=th_full[:, q, :], scalar=1.5,
                                                       in1=th_half[:, q, :], op0=ALU.mult, op1=ALU.add).then_inc(mix_ready, 1)
                        wait(dve, mix_ready, k + 1)
                        wait(dve, probs_ready, k - 1)
                        nc.vector.scalar_tensor_tensor(out=theta[:, q, :], in0=wide(bank, 2 * q), scalar=0.0,
                                                       in1=mix[:], op0=ALU.max, op1=ALU.add).then_inc(theta_ready, 1)
                        wait(dve, theta_ready, k + 1)
                        nc.vector.tensor_reduce(top[:, q:q + 1], theta[:, q, :], AX_X, ALU.max).then_inc(top_ready, 1)
                        wait(dve, top_ready, k + 1)
                        nc.vector.tensor_scalar(bias_top[:, q:q + 1], top[:, q:q + 1], -0.1, None,
                                                ALU.mult).then_inc(bias_ready, 1)
                        if m >= 2:
                            finish(m - 2)
                    finish(MT - 2)
                    finish(MT - 1)
            wait(dve, x_ready, B * MT)


def wide(bank, i):
    return bank(i, 0, 2 * BANK)


_INS = ['L0_attn_x', 'L0_attn_Wq', 'L0_attn_bq', 'L0_attn_Wk', 'L0_attn_bk', 'L0_attn_Wv', 'L0_attn_bv',
        'L0_attn_Wo', 'L0_attn_bo', 'L0_ffn_wqkv', 'L0_ffn_q_scale', 'L0_ffn_k_scale', 'L0_ffn_wo',
        'L0_ffn_ln_g', 'L0_ffn_ln_b', 'L0_ffn_w1', 'L0_ffn_b1', 'L0_ffn_w2', 'L0_ffn_b2']
_TRANSPOSED = ('L0_attn_Wq', 'L0_attn_Wk', 'L0_attn_Wv', 'L0_attn_Wo')


def kernel(**inputs):
    import concourse.bacc as bacc
    from concourse.bass_utils import run_bass_kernel_spmd

    nc = bacc.Bacc("TRN2", target_bir_lowering=False, num_devices=1)
    arrays, args = {}, []

    def declare(name, a):
        arrays[name] = a
        args.append(nc.dram_tensor(name, a.shape, mybir.dt.from_np(a.dtype), kind="ExternalInput").ap())

    for name in _INS:
        a = np.asarray(inputs[name])
        declare(f"in_{name}", np.ascontiguousarray(a.T if name in _TRANSPOSED else a))
    shape = inputs['L0_attn_x'].shape
    declare("rotary", rotary_tables(shape[1]))
    declare("masks", window_masks())
    declare("identity", np.eye(P, dtype=np.float32))
    args.append(nc.dram_tensor("out_0", shape, F32, kind="ExternalOutput").ap())
    macaron(nc, *args)
    r = run_bass_kernel_spmd(nc, [arrays], core_ids=[0])
    return r.results[0]["out_0"]
```

```python
from contextlib import ExitStack

import numpy as np

import concourse.bass as bass
from concourse import mybir

F32 = mybir.dt.float32
BF16 = mybir.dt.bfloat16
ACT = mybir.ActivationFunctionType
ALU = mybir.AluOpType
AX_X = mybir.AxisListType.X

P = 128
HEADS, DH, WIN = 8, 64, 64
INNER = HEADS * DH
HALF = P // 2
DEPTH = 2
HID = int(P * 4 * 2 / 3)
HID_CHUNKS = [(c, min(P, HID - c)) for c in range(0, HID, P)]
GROUP = 4
GCOLS = GROUP * P
QK_SCALE = 8.0
MASKED = -1e30
HD1 = DH + 1
BANK = 512
KT = WIN + P


def rotary_tables(n):
    half = np.arange(0, DH, 2, dtype=np.float32)
    inv_freq = (1.0 / (10000.0 ** (half / DH).astype(np.float64))).astype(np.float32)
    t = np.arange(n, dtype=np.float32)
    freqs = (t[:, None] * inv_freq[None, :]).astype(np.float64)
    base = ((half + 0.4 * DH) / (1.4 * DH)).astype(np.float32)
    power = (t - n // 2) / float(WIN // 2)
    scale = base[None, :].astype(np.float64) ** power[:, None].astype(np.float64)
    cos, sin = np.cos(freqs), np.sin(freqs)
    q, k = QK_SCALE * scale, 1.0 / scale
    pair = lambda a, b: np.concatenate([a, b], axis=-1)
    out = np.stack([pair(cos * q, cos * q), pair(cos * k, cos * k),
                    pair(-sin * q, sin * q), pair(-sin * k, sin * k)])
    return out.astype(np.float32)


def window_masks():
    i = np.arange(P)[:, None] % WIN
    j = np.arange(P)[None, :]
    open_ = (j >= i) & (j <= i + WIN)
    first = open_ & ((np.arange(P)[:, None] >= WIN) | (j >= WIN))
    return np.stack([np.tile(np.where(m, 0.0, MASKED), (1, 4)) for m in (first, open_)]).astype(np.float32)


class Tile:

    def __init__(self, row, n, g, m):
        self.row, self.n, self.g, self.m = row, n, g, m


class Group:

    def __init__(self, row, n, i, pairs, layer):
        self.row, self.n, self.i, self.pairs, self.layer = row, n, i, pairs, layer
        self.par = i // 2
        self.seq = 2 * pairs + self.par
        self.earlier = not isinstance(row, int) or row >= 1
        self.earlier2 = not isinstance(row, int) or row >= 2


class Query:

    def __init__(self, k, n, m, par):
        self.k, self.n, self.m, self.par = k, n, m, par


def macaron(nc, x_in, wq_in, bq_in, wk_in, bk_in, wv_in, bv_in, wo_in, bo_in,
            wqkv_in, qs_in, ks_in, fwo_in, lng_in, lnb_in, w1_in, b1_in, w2_in, b2_in,
            rot_in, mask_in, id_in, out):
    B, N, D = x_in.shape
    MT = N // P
    NT = B * MT
    NG = NT // GROUP
    x_rows = x_in.rearrange("b (m p) d -> b p m d", p=P)
    out_rows = out.rearrange("b (m p) d -> b p m d", p=P)

    with ExitStack() as whole:
        def keep(name, shape, dt=F32):
            return whole.enter_context(nc.sbuf_tensor(name, shape, dt))

        X = keep("X", [P, NT, D])
        Y = keep("Y", [P, NT, D])
        ident = keep("ident", [P, P])
        neg_half = keep("neg_half", [P, 16])
        ones_row = keep("ones_row", [1, P])
        psum = whole.enter_context(nc.psum_tensor("psum", [P, 8 * BANK], F32))

        held = {}

        def sems(name):
            if name not in held:
                held[name] = whole.enter_context(nc.semaphore(name))
            return held[name]

        def bank(i, lo=0, hi=BANK, rows=slice(0, P)):
            return psum[rows, i * BANK + lo:i * BANK + hi]

        load_and_constants(nc, sems, X, ident, neg_half, ones_row, x_rows, id_in, B, MT)
        for call in range(2):
            layer_norm(nc, sems, f"pre{call}", X, Y, neg_half, B, MT)
            feed_forward(nc, sems, call, Y, ident, neg_half, ones_row, psum, bank, B, MT,
                         wqkv_in, qs_in, ks_in, fwo_in, lng_in, lnb_in, w1_in, b1_in, w2_in, b2_in,
                         rot_in, mask_in)
            add_half(nc, sems, f"half{call}", X, Y, B, MT, out_rows if call else None)
            if call == 0:
                layer_norm(nc, sems, "att", X, Y, neg_half, B, MT)
                attention(nc, sems, X, Y, ident, ones_row, bank, B, MT,
                          wq_in, bq_in, wk_in, bk_in, wv_in, bv_in, wo_in, bo_in)


def wait(engine, semaphore, value):
    if value is not None and not (isinstance(value, int) and value <= 0):
        engine.wait_ge(semaphore, value)


def load_and_constants(nc, sems, X, ident, neg_half, ones_row, x_rows, id_in, B, MT):
    with ExitStack() as ctx:
        loaded = sems("loaded")
        consts = sems("consts")
        block = ctx.enter_context(nc.Block())

        @block.sync
        def _(sp):
            for b in range(B):
                sp.dma_start(X[:, b * MT:(b + 1) * MT, :], x_rows[b]).then_inc(loaded, 16)
            sp.dma_start(ident[:], id_in).then_inc(loaded, 16)
            sp.wait_ge(loaded, 16 * (B + 1))

        @block.vector
        def _(dve):
            nc.vector.memset(neg_half[:], -0.5).then_inc(consts, 1)
            nc.vector.memset(ones_row[:], 1.0).then_inc(consts, 1)
            dve.wait_ge(consts, 2)


def layer_norm(nc, sems, name, src, dst, neg_half, B, MT):
    with ExitStack() as ctx:
        sem = lambda n: sems(f"{name}_{n}")
        sb = lambda n, s: ctx.enter_context(nc.sbuf_tensor(f"{name}_{n}", s, F32))
        stats = sb("stats", [P, 2, MT, 6])
        mean_var = sb("mean_var", [P, 2, MT, 2])
        rstd = sb("rstd", [P, 2, MT])
        stats_done, var_done, var_eps, rstd_done, normed = map(
            sem, ("stats_done", "var_done", "var_eps", "rstd_done", "normed"))
        block = ctx.enter_context(nc.Block())

        @block.gpsimd
        def _(pool):
            for b in range(B):
                pool.wait_ge(var_eps, b + 1)
                nc.gpsimd.tensor_tensor(rstd[:, b % 2, :], rstd[:, b % 2, :], neg_half[:, 0:MT],
                                        ALU.pow).then_inc(rstd_done, 1)

        @block.vector
        def _(dve):
            def statistics(b):
                if b >= 2:
                    dve.wait_ge(normed, MT * (b - 1))
                for m in range(MT):
                    nc.vector.bn_stats(stats[:, b % 2, m, :], src[:, b * MT + m, :]).then_inc(stats_done, 1)
                dve.wait_ge(stats_done, MT * (b + 1))
                for m in range(MT):
                    nc.vector.bn_aggr(mean_var[:, b % 2, m, :], stats[:, b % 2, m, :]).then_inc(var_done, 1)
                dve.wait_ge(var_done, MT * (b + 1))
                nc.vector.tensor_scalar_add(rstd[:, b % 2, :], mean_var[:, b % 2, :, 1], 1e-5).then_inc(var_eps, 1)

            def normalise(b):
                dve.wait_ge(rstd_done, b + 1)
                for m in range(MT):
                    nc.vector.tensor_scalar(dst[:, b * MT + m, :], src[:, b * MT + m, :],
                                            mean_var[:, b % 2, m, 0:1], rstd[:, b % 2, m:m + 1],
                                            ALU.subtract, ALU.mult).then_inc(normed, 1)

            statistics(0)
            for b in range(B):
                if b + 1 < B:
                    statistics(b + 1)
                normalise(b)
            dve.wait_ge(normed, MT * B)


def add_half(nc, sems, name, X, Y, B, MT, out_rows):
    with ExitStack() as ctx:
        added = sems(f"{name}_added")
        stored = sems(f"{name}_stored")
        block = ctx.enter_context(nc.Block())

        @block.vector
        def _(dve):
            for b in range(B):
                xs, ys = (t[:, b * MT:(b + 1) * MT, :].rearrange("p m d -> p (m d)") for t in (X, Y))
                nc.vector.scalar_tensor_tensor(out=xs, in0=ys, scalar=0.5, in1=xs, op0=ALU.mult,
                                               op1=ALU.add).then_inc(added, 1)
            dve.wait_ge(added, B)

        if out_rows is not None:
            @block.sync
            def _(sp):
                for b in range(B):
                    sp.wait_ge(added, b + 1)
                    sp.dma_start(out_rows[b], X[:, b * MT:(b + 1) * MT, :]).then_inc(stored, 16)
                sp.wait_ge(stored, 16 * B)


def feed_forward(nc, sems, call, Y, ident, neg_half, ones_row, psum, bank, B, MT,
                 wqkv_in, qs_in, ks_in, wo_in, lng_in, lnb_in, w1_in, b1_in, w2_in, b2_in,
                 rot_in, mask_in):
    NT = B * MT
    assert MT == 8 and GROUP == 4
    name = "ffn"
    with ExitStack() as ctx:
        sb = lambda n, s, dt=F32: ctx.enter_context(nc.sbuf_tensor(f"{name}{call}_{n}", s, dt))
        sem = lambda n: sems(f"{name}_{n}")

        wqkv = sb("wqkv", [P, 3 * INNER])
        wo = sb("wo", [P, INNER // P, P])
        w1 = sb("w1", [P, 2 * HID])
        w1g = sb("w1g", [P, 2 * HID])
        w2 = sb("w2", [P, len(HID_CHUNKS), P])
        b1 = sb("b1", [P, 2, len(HID_CHUNKS)])
        b1g = sb("b1g", [P, 2, len(HID_CHUNKS)])
        lng = sb("lng", [P, 1])
        lnb = sb("lnb", [P, 1])
        qks = sb("qks", [P, 2, DH])
        rot = sb("rot", [P, 4, MT, DH])
        cos = sb("cos", [P, MT, 2, DH])
        sin = sb("sin", [P, MT, 2, DH])
        mask = sb("mask", [P, 2, BANK], BF16)
        ident16 = sb("ident16", [P, P], BF16)
        ystage = sb("ystage", [P, 4, P])
        hT = sb("hT", [P, MT * P + 1])
        sq = sb("sq", [P, 2 * INNER])
        ssq = sb("ssq", [P, 16])
        ssq_floor = sb("ssq_floor", [P, 16])
        rnorm = sb("rnorm", [P, 16])
        qkn = sb("qkn", [P, 2 * INNER])
        qk_cos = sb("qk_cos", [P, 2 * INNER])
        qk_sin = sb("qk_sin", [P, 2 * INNER])
        qkr = sb("qkr", [P, 2 * INNER])
        qT = sb("qT", [P, 2, 4, P])
        kT = sb("kT", [P, 2, 4, KT])
        v = sb("v", [P, 4, HEADS, HD1])
        vprev = sb("vprev", [P, 4, HEADS, HD1])
        neg_max = sb("neg_max", [P, HEADS])
        probs = sb("probs", [P, HEADS * P])
        mask32 = probs[:].rearrange("p (t c) -> p t c", t=2)
        probsT = sb("probsT", [P, HEADS * P])
        rsum = sb("rsum", [P, HEADS])
        o = sb("o", [P, INNER])
        oT = sb("oT", [P, INNER])
        h = sb("h", [P, 2, MT, P])
        stats = sb("stats", [P, MT, 6])
        half_even, mean, half_diff, half_diff_sq, spread, spread_eps = (
            sb(n, [P, MT]) for n in ("half_even", "mean", "half_diff", "half_diff_sq", "spread", "spread_eps"))
        var_eps = sb("var_eps", [P, MT])
        rstd = sb("rstd", [P, MT])
        z = sb("z", [P, 2, GROUP, P])
        zT = sb("zT", [P, GCOLS])
        gate = sb("gate", [P, len(HID_CHUNKS), GCOLS])
        hid = sb("hid", [P, 2, len(HID_CHUNKS), GCOLS])

        (consts_in, consts_done, w_in, scales_in, b1_psum, tables_ready, w1g_ready, b1_ready,
         staged_T, hT_ready, qk_psum, qkv_ready, sq_ready, v_ready, ssq_ready, floor_ready,
         rnorm_ready, qkn_ready, cos_ready, sin_ready, qkr_ready, qkT_psum, qkT_ready,
         scores_ready, max_ready, probs_ready, probsT_psum, probsT_ready,
         pv_ready, rsum_ready, o_ready, oT_psum, oT_ready, attn_ready, x1_ready, 
         stats_ready, var_ready, eps_ready, rstd_ready, z_ready, zT_psum, zT_ready, ag_psum,
         gate_ready, hid_ready, mlp_ready, y_ready) = map(sem, """consts_in consts_done w_in scales_in
         b1_psum tables_ready w1g_ready b1_ready staged_T hT_ready qk_psum qkv_ready sq_ready
         v_ready ssq_ready floor_ready rnorm_ready qkn_ready cos_ready sin_ready qkr_ready
         qkT_psum qkT_ready scores_ready max_ready probs_ready probsT_psum probsT_ready
         pv_ready rsum_ready o_ready oT_psum oT_ready attn_ready x1_ready stats_ready
         var_ready eps_ready rstd_ready z_ready zT_psum zT_ready ag_psum gate_ready hid_ready
         mlp_ready y_ready""".split())

        staged = [sem(f"staged{i}") for i in range(4)]
        vprev_ready = [sem(f"vprev_ready{i}") for i in range(4)]
        layer_over = sem("layer_over")
        h_in = [sem(f"h_in{i}") for i in range(2)]
        heads = lambda t: t.rearrange("p (h d) -> p h d", d=DH)
        NG = NT // GROUP

        def layers(engine, start, slot, mlp_slot, over=None):
            with engine.Fori(DEPTH * call, DEPTH * call + DEPTH) as l:
                start(l)

                def tiles_at(s):
                    def tile(d):
                        n = s + d
                        return Tile(n, l * NT + n, l * NG + n // GROUP, n % MT) if 0 <= n < NT else None
                    return tile

                def tiles_in(b, j):
                    def tile(d):
                        n = j + d
                        return Tile(b * MT + n, l * NT + b * MT + n,
                                    l * NG + b * (MT // GROUP) + n // GROUP, n % MT)
                    return tile

                for s in range(-3, MT):
                    slot(tiles_at(s))
                with engine.Fori(1, B - 1) as b:
                    for j in range(MT):
                        slot(tiles_in(b, j))
                for s in range(NT - MT, NT + 1):
                    slot(tiles_at(s))

                def groups_at(s):
                    def group(d):
                        n = s + d
                        return Group(n, l * NG + n, n % 4, l * (B // 2) + n // 4, l) if 0 <= n < NG else None
                    return group

                def groups_in(pair, j):
                    def group(d):
                        n = j + d
                        return Group(pair * 4 + n, l * NG + pair * 4 + n, n % 4, l * (B // 2) + pair + n // 4, l)
                    return group

                for s in range(-4, 4):
                    mlp_slot(s, groups_at(s))
                with engine.Fori(1, B // 2 - 1) as pair:
                    for j in range(4):
                        mlp_slot(j, groups_in(pair, j))
                for s in range(NG - 4, NG + 2):
                    mlp_slot(s, groups_at(s))
                engine.wait_ge(y_ready, (l + 1) * NG)
                if over is not None:
                    engine.sem_inc(over, 1)

        def before(t, k, times=1):
            local = t.row + 1 - k if isinstance(t.row, int) else 1
            return None if local <= 0 else times * (t.n + 1 - k)

        block = ctx.enter_context(nc.Block())

        @block.sync
        def _(sp):
            sp.dma_start(rot[:], rot_in.rearrange("t (m p) d -> p t m d", p=P)).then_inc(consts_in, 16)
            sp.dma_start(mask32, mask_in.rearrange("t p c -> p t c")).then_inc(consts_in, 16)

            def start(l):
                row = lambda t: t[bass.ds(l - DEPTH * call, 1), :]
                sp.dma_start(qks[:, 0, :], row(qs_in).partition_broadcast(P)).then_inc(scales_in, 16)
                sp.dma_start(qks[:, 1, :], row(ks_in).partition_broadcast(P)).then_inc(scales_in, 16)
                sp.dma_start(wqkv[:], wqkv_in[bass.ds(l - DEPTH * call, 1)].rearrange("o d n -> d (o n)")).then_inc(w_in, 16)
                sp.dma_start(wo[:], wo_in[bass.ds(l - DEPTH * call, 1)].rearrange("o (c p) n -> p (o c) n", p=P)).then_inc(w_in, 16)
                sp.dma_start(w1[:], w1_in[bass.ds(l - DEPTH * call, 1)].rearrange("o d n -> d (o n)")).then_inc(w_in, 16)
                for c, (lo, size) in enumerate(HID_CHUNKS):
                    sp.dma_start(w2[0:size, c, :], w2_in[bass.ds(l - DEPTH * call, 1), lo:lo + size, :].rearrange(
                        "o p n -> p (o n)")).then_inc(w_in, 16)
                    for half in range(2):
                        sp.dma_start(b1[0:size, half, c:c + 1],
                                     b1_in[bass.ds(l - DEPTH * call, 1), half * HID + lo:half * HID + lo + size]
                                     .rearrange("o p -> p o")).then_inc(w_in, 16)
                sp.dma_start(w2[size:size + 1, c, :], row(b2_in)).then_inc(w_in, 16)
                sp.dma_start(lng[:], row(lng_in).rearrange("o p -> p o")).then_inc(w_in, 16)
                sp.dma_start(lnb[:], row(lnb_in).rearrange("o p -> p o")).then_inc(w_in, 16)

            def slot(tile):
                if t := tile(3):
                    row = t.row if isinstance(t.row, int) else sp.snap(t.row)
                    wait(sp, staged_T, before(t, 4))
                    sp.dma_start(ystage[:, t.m % 4, :], Y[:, bass.ds(row, 1), :]
                                 .rearrange("p o d -> p (o d)")).then_inc(staged[t.m % 4], 16)
                if t := tile(2):
                    wait(sp, v_ready, before(t, 0))
                    sp.dma_start(vprev[WIN:P, t.m % 4], v[0:WIN, t.m % 4]).then_inc(vprev_ready[t.m % 4], 16)
                    lo = v[WIN:P, (t.m - 1) % 4] if t.m else v[0:WIN, 0]
                    sp.dma_start(vprev[0:WIN, t.m % 4], lo).then_inc(vprev_ready[t.m % 4], 16)

            def mlp_slot(s, group):
                if s % 2 == 0 and (t := group(4)):
                    rows = t.row * GROUP if isinstance(t.row, int) else sp.snap(t.row * GROUP)
                    if not (isinstance(t.row, int) and t.row < 4):
                        sp.wait_ge(z_ready, GROUP * (t.n - 2))
                    wait(sp, x1_ready, GROUP * (t.n + 2))
                    dst, src = h[:, t.par], Y[:, bass.ds(rows, MT), :]
                    sp.dma_start(dst[:, :, 0:HALF], src[:, :, 0:HALF]).then_inc(h_in[t.par], 16)
                    sp.dma_start(dst[1:P, :, HALF:P], src[0:P - 1, :, HALF:P]).then_inc(h_in[t.par], 16)
                    sp.dma_start(dst[0:1, 1:MT, HALF:P], src[P - 1:P, 0:MT - 1, HALF:P]).then_inc(h_in[t.par], 16)

            sp.wait_ge(consts_done, 6 * call + 6)
            layers(sp, start, slot, mlp_slot, layer_over)

        @block.gpsimd
        def _(pool):
            def slot(tile):
                if t := tile(2):
                    wait(pool, floor_ready, before(t, 0))
                    wait(pool, qkn_ready, before(t, 1))
                    nc.gpsimd.tensor_tensor(rnorm[:], ssq_floor[:], neg_half[:], ALU.pow).then_inc(rnorm_ready, 1)
                    wait(pool, qkn_ready, before(t, 0))
                    wait(pool, qkr_ready, before(t, 1))
                    x = qkn[:].rearrange("p (t h e d) -> p t h e d", t=2, h=HEADS, e=2)
                    y = qk_sin[:].rearrange("p (t h e d) -> p t h e d", t=2, h=HEADS, e=2)
                    s = sin[:, t.m].rearrange("p t (e d) -> p t e d", e=2)
                    for e in range(2):
                        nc.gpsimd.tensor_tensor(
                            y[:, :, :, e, :], x[:, :, :, 1 - e, :],
                            s[:, :, e, :].unsqueeze(2).to_broadcast([P, 2, HEADS, DH // 2]),
                            ALU.mult).then_inc(sin_ready, 1)

            def start(l):
                pool.wait_ge(tables_ready, 4 * l + 4)

            def mlp_slot(s, group):
                if s % 2 == 0 and (t := group(2)):
                    pool.wait_ge(eps_ready, t.seq + 1)
                    nc.gpsimd.tensor_tensor(rstd[:], var_eps[:], neg_half[:, 0:MT], ALU.pow).then_inc(rstd_ready, 1)

            layers(pool, start, slot, mlp_slot)

        @block.scalar
        def _(act):
            def start(l):
                act.wait_ge(b1_ready, 2 * l + 2)

            def slot(tile):
                if t := tile(-1):
                    wait(act, oT_psum, before(t, 0))
                    wait(act, attn_ready, before(t, 1))
                    nc.scalar.copy(oT[:], bank(5)).then_inc(oT_ready, 1)
                if t := tile(0):
                    for i in range(2):
                        act.wait_ge(max_ready, 2 * t.n + i + 1)
                        wait(act, probsT_psum, before(t, 1, 2))
                        for c in range(4):
                            last = nc.scalar.activation(probs[:, (4 * i + c) * P:(4 * i + c + 1) * P],
                                                        bank(3 + i, c * P, (c + 1) * P), ACT.Exp,
                                                        bias=neg_max[:, 4 * i + c:4 * i + c + 1])
                        last.then_inc(probs_ready, 1)
                if t := tile(2):
                    wait(act, qk_psum, before(t, 0))
                    wait(act, ssq_ready, before(t, 1))
                    nc.scalar.activation(sq[:], psum[:, 0:2 * BANK], ACT.Square).then_inc(sq_ready, 1)
                    wait(act, qkv_ready, before(t, 0))
                    wait(act, pv_ready, before(t, 4))
                    if u := tile(-1):
                        act.wait_ge(vprev_ready[u.m % 4], 32 * (u.g + 1))
                    nc.scalar.copy(v[:, t.m % 4, :, 0:DH], heads(bank(2))).then_inc(v_ready, 1)
                if t := tile(3):
                    wait(act, staged_T, before(t, 0))
                    wait(act, qkv_ready, before(t, MT - 1))
                    nc.scalar.copy(hT[0:HALF, t.m * P:(t.m + 1) * P], bank(7, 384, 512, slice(0, HALF))).then_inc(hT_ready, 1)
                    nc.scalar.copy(hT[HALF:P, t.m * P + 1:(t.m + 1) * P + 1],
                                   bank(7, 384, 512, slice(HALF, P))).then_inc(hT_ready, 1)
                if t := tile(0):
                    for i in range(2):
                        cols = slice(i * BANK, (i + 1) * BANK)
                        act.wait_ge(probsT_psum, 2 * t.n + i + 1)
                        wait(act, pv_ready, before(t, 1))
                        nc.scalar.copy(probsT[:, cols], bank(3 + i)).then_inc(probsT_ready, 1)
                if t := tile(1):
                    wait(act, qkT_psum, before(t, 0))
                    wait(act, scores_ready, before(t, 1))
                    nc.scalar.copy(qT[:, t.m % 2].rearrange("p c n -> p (c n)"), bank(5)).then_inc(qkT_ready, 1)
                    src = bank(6).rearrange("p (c n) -> p c n", n=P)
                    nc.scalar.copy(kT[:, t.m % 2, :, WIN:KT], src).then_inc(qkT_ready, 1)
                    nc.scalar.copy(kT[:, (t.m + 1) % 2, :, 0:WIN], src[:, :, WIN:P]).then_inc(qkT_ready, 1)

            def mlp_slot(s, group):
                if t := group(0):
                    for c, (lo, size) in enumerate(HID_CHUNKS):
                        act.wait_ge(ag_psum, 3 * t.n + c + 1)
                        if t.earlier:
                            act.wait_ge(hid_ready, 3 * t.n + c - 2)
                        nc.scalar.activation(gate[0:size, c, :], bank(2 * c + 1, rows=slice(0, size)),
                                             ACT.Gelu, bias=b1g[0:size, 1, c:c + 1]).then_inc(gate_ready, 1)
                if t := group(1):
                    act.wait_ge(zT_psum, t.n + 1)
                    nc.scalar.copy(zT[:], bank(7)).then_inc(zT_ready, 1)

            layers(act, start, slot, mlp_slot)

        @block.vector
        def _(dve):
            nc.vector.memset(v[:, :, :, DH:HD1], 1.0).then_inc(consts_done, 1)
            nc.vector.memset(hT[HALF:P, 0:1], 0.0).then_inc(consts_done, 1)
            nc.vector.memset(h[0:1, :, 0, HALF:P], 0.0).then_inc(consts_done, 1)
            nc.vector.memset(hid[:, :, len(HID_CHUNKS) - 1, :], 1.0).then_inc(consts_done, 1)
            nc.vector.tensor_copy(ident16[:], ident[:]).then_inc(consts_done, 1)
            dve.wait_ge(consts_in, 32 * call + 32)
            nc.vector.tensor_copy(mask[:], mask32).then_inc(consts_done, 1)

            def start(l):
                dve.wait_ge(scales_in, 32 * (l + 1))
                for t in range(2):
                    nc.vector.tensor_tensor(cos[:, :, t, :], rot[:, t], qks[:, t:t + 1, :].to_broadcast([P, MT, DH]),
                                            ALU.mult).then_inc(tables_ready, 1)
                for e in range(2):
                    for t in range(2):
                        lo, other = e * (DH // 2), (1 - e) * (DH // 2)
                        ins = nc.vector.tensor_tensor(
                            sin[:, :, t, lo:lo + DH // 2], rot[:, 2 + t, :, lo:lo + DH // 2],
                            qks[:, t:t + 1, other:other + DH // 2].to_broadcast([P, MT, DH // 2]), ALU.mult)
                        if e == 1:
                            ins.then_inc(tables_ready, 1)
                dve.wait_ge(w_in, 16 * 15 * (l + 1))
                nc.vector.tensor_scalar(w1g[:], w1[:], lng[:, 0:1], None, ALU.mult).then_inc(w1g_ready, 1)
                dve.wait_ge(b1_psum, l + 1)
                pb = bank(7, 0, 6).rearrange("p (h c) -> p h c", h=2)
                nc.vector.tensor_tensor(b1g[:, :, 0:2], b1[:, :, 0:2], pb[:, :, 0:2], ALU.add).then_inc(b1_ready, 1)
                last = HID_CHUNKS[-1][1]
                nc.vector.tensor_tensor(b1g[0:last, :, 2:3], b1[0:last, :, 2:3], pb[0:last, :, 2:3],
                                        ALU.add).then_inc(b1_ready, 1)

            def slot(tile):
                if t := tile(0):
                    for i in range(2):
                        s = bank(3 + i).rearrange("p (h k) -> p h k", k=P)
                        wait(dve, scores_ready, before(t, 0))
                        wait(dve, probs_ready, before(t, 1, 2))
                        nc.vector.tensor_reduce(neg_max[:, 4 * i:4 * i + 4], s, AX_X, ALU.max,
                                                negate=True).then_inc(max_ready, 1)
                if t := tile(1):
                    wait(dve, qkn_ready, before(t, 0))
                    wait(dve, qkr_ready, before(t, 1))
                    nc.vector.tensor_tensor(
                        qk_cos[:].rearrange("p (t h d) -> p t h d", t=2, d=DH),
                        qkn[:].rearrange("p (t h d) -> p t h d", t=2, d=DH),
                        cos[:, t.m].unsqueeze(2).to_broadcast([P, 2, HEADS, DH]),
                        ALU.mult).then_inc(cos_ready, 1)
                if t := tile(1):
                    wait(dve, sin_ready, before(t, 0, 2))
                    wait(dve, cos_ready, before(t, 0))
                    wait(dve, qkT_psum, before(t, 1))
                    nc.vector.tensor_tensor(qkr[:], qk_cos[:], qk_sin[:], ALU.add).then_inc(qkr_ready, 1)
                if t := tile(-1):
                    wait(dve, attn_ready, before(t, 0))
                    y = Y[:, bass.ds(t.row, 1), :].rearrange("p o d -> p (o d)")
                    nc.vector.tensor_tensor(y, bank(6, 0, P), y, ALU.add).then_inc(x1_ready, 1)
                if t := tile(2):
                    wait(dve, sq_ready, before(t, 0))
                    nc.vector.tensor_reduce(ssq[:], sq[:].rearrange("p (h d) -> p h d", d=DH), AX_X,
                                            ALU.add).then_inc(ssq_ready, 1)
                    wait(dve, ssq_ready, before(t, 0))
                    wait(dve, rnorm_ready, before(t, 1))
                    nc.vector.tensor_scalar_max(ssq_floor[:], ssq[:], 1e-24).then_inc(floor_ready, 1)
                if t := tile(0):
                    wait(dve, pv_ready, before(t, 0))
                    wait(dve, o_ready, before(t, 1, 2))
                    for i, bk in enumerate((7, 2)):
                        pv = bank(bk, 0, 4 * HD1).rearrange("p (h d) -> p h d", d=HD1)
                        nc.vector.reciprocal(rsum[:, 4 * i:4 * i + 4], pv[:, :, DH]).then_inc(rsum_ready, 1)
                    dve.wait_ge(rsum_ready, 2 * t.n + 2)
                    wait(dve, oT_psum, before(t, 1))
                    for i, bk in enumerate((7, 2)):
                        pv = bank(bk, 0, 4 * HD1).rearrange("p (h d) -> p h d", d=HD1)
                        nc.vector.tensor_tensor(
                            heads(o[:])[:, 4 * i:4 * i + 4, :], pv[:, :, 0:DH],
                            rsum[:, 4 * i:4 * i + 4].unsqueeze(2).to_broadcast([P, 4, DH]),
                            ALU.mult).then_inc(o_ready, 1)
                if t := tile(2):
                    wait(dve, rnorm_ready, before(t, 0))
                    wait(dve, sin_ready, before(t, 1, 2))
                    wait(dve, cos_ready, before(t, 1))
                    nc.vector.tensor_tensor(heads(qkn[:]), heads(psum[:, 0:2 * BANK]),
                                            rnorm[:].unsqueeze(2).to_broadcast([P, 16, DH]),
                                            ALU.mult).then_inc(qkn_ready, 1)

            def mlp_slot(s, group):
                if t := group(1):
                    if (t.i % 2) == 0:
                        dve.wait_ge(rstd_ready, t.seq + 1)
                    if t.earlier2:
                        dve.wait_ge(zT_psum, t.n - 1)
                    for k in range(GROUP):
                        m = (t.i % 2) * GROUP + k
                        nc.vector.tensor_scalar(z[:, t.i % 2, k, :], h[:, t.par, m, :], mean[:, m:m + 1],
                                                rstd[:, m:m + 1], ALU.subtract, ALU.mult).then_inc(z_ready, 1)
                if t := group(-2):
                    dve.wait_ge(mlp_ready, t.n + 1)
                    y = Y[:, bass.ds(t.row * GROUP, GROUP), :].rearrange("p m d -> p (m d)")
                    nc.vector.tensor_tensor(y, bank(6), y, ALU.add).then_inc(y_ready, 1)
                if t := group(0):
                    for c, (lo, size) in enumerate(HID_CHUNKS):
                        dve.wait_ge(gate_ready, 3 * t.n + c + 1)
                        if t.earlier2:
                            dve.wait_ge(mlp_ready, t.n - 1)
                        nc.vector.scalar_tensor_tensor(
                            out=hid[0:size, t.i % 2, c, :], in0=bank(2 * c, rows=slice(0, size)),
                            scalar=b1g[0:size, 0, c:c + 1], in1=gate[0:size, c, :],
                            op0=ALU.add, op1=ALU.mult).then_inc(hid_ready, 1)
                if s % 2 == 0 and (t := group(2)):
                    dve.wait_ge(h_in[t.par], 48 * (t.pairs + 1))
                    for m in range(MT):
                        nc.vector.bn_stats(stats[:, m, :], h[:, t.par, m, :]).then_inc(stats_ready, 1)
                    dve.wait_ge(stats_ready, MT * (t.seq + 1))
                    me, se, mo, so = (stats[:, :, i] for i in (1, 2, 4, 5))
                    nc.vector.tensor_scalar(half_even[:], me, 0.5, None, ALU.mult).then_inc(var_ready, 1)
                    nc.vector.tensor_tensor(spread[:], se, so, ALU.add).then_inc(var_ready, 1)
                    dve.wait_ge(var_ready, 6 * t.seq + 2)
                    nc.vector.scalar_tensor_tensor(out=mean[:], in0=mo, scalar=0.5, in1=half_even[:],
                                                   op0=ALU.mult, op1=ALU.add).then_inc(var_ready, 1)
                    nc.vector.scalar_tensor_tensor(out=half_diff[:], in0=mo, scalar=-0.5, in1=half_even[:],
                                                   op0=ALU.mult, op1=ALU.add).then_inc(var_ready, 1)
                    nc.vector.tensor_scalar(spread_eps[:], spread[:], 1.0 / P, 1e-5, ALU.mult, ALU.add).then_inc(var_ready, 1)
                    dve.wait_ge(var_ready, 6 * t.seq + 5)
                    nc.vector.tensor_tensor(half_diff_sq[:], half_diff[:], half_diff[:], ALU.mult).then_inc(var_ready, 1)
                    dve.wait_ge(var_ready, 6 * t.seq + 6)
                    nc.vector.tensor_tensor(var_eps[:], half_diff_sq[:], spread_eps[:], ALU.add).then_inc(eps_ready, 1)

            layers(dve, start, slot, mlp_slot)

        @block.tensor
        def _(pe):
            def start(l):
                pe.wait_ge(w_in, 16 * 15 * (l + 1))
                for half in range(2):
                    for c, (lo, size) in enumerate(HID_CHUNKS):
                        col = half * 3 + c
                        last = nc.tensor.matmul(bank(7, col, col + 1, slice(0, size)),
                                                w1[:, half * HID + lo:half * HID + lo + size], lnb[:, 0:1],
                                                start=True, stop=True)
                last.then_inc(b1_psum, 1)
                pe.wait_ge(b1_ready, 2 * l + 2)
                pe.wait_ge(w1g_ready, l + 1)
                pe.wait_ge(consts_done, 6 * call + 6)

            def mlp_slot(s, group):
                if t := group(0):
                    pe.wait_ge(zT_ready, t.n + 1)
                    for c, (lo, size) in enumerate(HID_CHUNKS):
                        if t.earlier:
                            pe.wait_ge(hid_ready, 3 * t.n + c - 2)
                        for half in range(2):
                            last = nc.tensor.matmul(bank(2 * c + half, rows=slice(0, size)),
                                                    w1g[:, half * HID + lo:half * HID + lo + size], zT[:],
                                                    start=True, stop=True)
                        last.then_inc(ag_psum, 1)
                if t := group(1):
                    pe.wait_ge(z_ready, GROUP * (t.n + 1))
                    if t.earlier:
                        pe.wait_ge(zT_ready, t.n)
                    else:
                        pe.wait_ge(x1_ready, NT * (t.layer + 1))
                    for k in range(GROUP):
                        last = nc.tensor.transpose(bank(7, k * P, (k + 1) * P), z[:, t.i % 2, k, :], ident[:])
                    last.then_inc(zT_psum, 1)
                if t := group(-1):
                    pe.wait_ge(hid_ready, 3 * t.n + 3)
                    if t.earlier:
                        pe.wait_ge(y_ready, t.n)
                    for k in range(GROUP):
                        for c, (lo, size) in enumerate(HID_CHUNKS):
                            rows = size if c < len(HID_CHUNKS) - 1 else size + 1
                            last = nc.tensor.matmul(bank(6, k * P, (k + 1) * P),
                                                    hid[0:rows, t.i % 2, c, k * P:(k + 1) * P], w2[0:rows, c, :],
                                                    start=(c == 0), stop=(c == len(HID_CHUNKS) - 1))
                    last.then_inc(mlp_ready, 1)

            def scores(t):
                wait(pe, qkT_ready, before(t, 0, 3))
                wait(pe, probsT_ready, before(t, 1, 2))
                for i in range(2):
                    nc.tensor.matmul(bank(3 + i), ident16[:], mask[:, 1 if t.m else 0, :],
                                     start=True, stop=False, skip_group_check=True)
                lo = 0 if t.m else WIN
                for hh in range(4):
                    for i in range(2):
                        rows = slice(DH * i, DH * i + DH)
                        q = qT[rows, t.m % 2, hh, :]
                        k = kT[rows, t.m % 2, hh, :]
                        nc.tensor.matmul(bank(3 + i, hh * P + lo, (hh + 1) * P, slice(0, WIN)), q[:, 0:WIN],
                                         k[:, lo:P], start=False, stop=True, skip_group_check=True)
                        last = nc.tensor.matmul(bank(3 + i, hh * P, (hh + 1) * P, slice(WIN, P)), q[:, WIN:P],
                                                k[:, WIN:KT], start=False, stop=True, skip_group_check=True)
                last.then_inc(scores_ready, 1)

            def heads_transpose(t):
                wait(pe, o_ready, before(t, 0, 2))
                for c in range(INNER // P):
                    last = nc.tensor.transpose(bank(5, c * P, (c + 1) * P), o[:, c * P:(c + 1) * P], ident[:])
                last.then_inc(oT_psum, 1)

            def project_qk(t):
                wait(pe, hT_ready, before(t, 0, 2))
                wait(pe, qkn_ready, before(t, 1))
                for i in range(2):
                    last = nc.tensor.matmul(bank(i), hT[:, t.m * P:(t.m + 1) * P],
                                            wqkv[:, i * INNER:(i + 1) * INNER], start=True, stop=True)
                last.then_inc(qk_psum, 1)

            def project_v(t, u):
                wait(pe, v_ready, before(t, 1))
                if u:
                    wait(pe, o_ready, before(u, 0, 2))
                nc.tensor.matmul(bank(2), hT[:, t.m * P:(t.m + 1) * P], wqkv[:, 2 * INNER:3 * INNER],
                                 start=True, stop=True).then_inc(qkv_ready, 1)

            def project_out(t):
                wait(pe, oT_ready, before(t, 0))
                for c in range(INNER // P):
                    last = nc.tensor.matmul(bank(6, 0, P), oT[:, c * P:(c + 1) * P], wo[:, c, :],
                                            start=(c == 0), stop=(c == INNER // P - 1))
                last.then_inc(attn_ready, 1)

            def tokens_transpose(t):
                pe.wait_ge(staged[t.m % 4], 16 * (t.g + 1))
                wait(pe, hT_ready, before(t, 1, 2))
                nc.tensor.transpose(bank(7, 384, 512), ystage[:, t.m % 4, :], ident[:]).then_inc(staged_T, 1)

            def weights_transpose(t):
                for i in range(2):
                    pe.wait_ge(probs_ready, 2 * t.n + i + 1)
                    for c in range(4 * i, 4 * i + 4):
                        last = nc.tensor.transpose(bank(3 + i, (c % 4) * P, (c % 4 + 1) * P),
                                                   probs[:, c * P:(c + 1) * P], ident[:])
                    last.then_inc(probsT_psum, 1)

            def rotated_transpose(t, u):
                wait(pe, qkr_ready, before(t, 0))
                if u:
                    wait(pe, x1_ready, before(u, 0))
                else:
                    wait(pe, qkT_ready, before(t, 1, 3))
                for c in range(8):
                    last = nc.tensor.transpose(bank(5 + c // 4, (c % 4) * P, (c % 4 + 1) * P),
                                               qkr[:, c * P:(c + 1) * P], ident[:])
                last.then_inc(qkT_psum, 1)

            def weigh_values(t):
                pe.wait_ge(vprev_ready[t.m % 4], 32 * (t.g + 1))
                wait(pe, o_ready, before(t, 1, 2))
                pe.wait_ge(probsT_ready, 2 * t.n + 2)
                for h in range(HEADS):
                    at_h = (h % 2) * BANK + (h // 2) * P
                    col = (h % 4) * HD1
                    lo = 0 if t.m else WIN
                    bk = (7, 2)[h // 4]
                    nc.tensor.matmul(bank(bk, col, col + HD1, slice(WIN, P)),
                                     probsT[:, at_h + WIN:at_h + P], v[:, t.m % 4, h, :],
                                     start=True, stop=True)
                    last = nc.tensor.matmul(bank(bk, col, col + HD1, slice(0, WIN)),
                                            probsT[lo:P, at_h:at_h + WIN], vprev[lo:P, t.m % 4, h, :],
                                            start=True, stop=True)
                last.then_inc(pv_ready, 1)

            def slot(tile):
                done, now, soon, next_, last_ = tile(-1), tile(0), tile(1), tile(2), tile(3)
                if now:
                    scores(now)
                if done:
                    heads_transpose(done)
                if next_:
                    project_qk(next_)
                    project_v(next_, done)
                if last_:
                    tokens_transpose(last_)
                if done:
                    project_out(done)
                if now:
                    weights_transpose(now)
                if soon:
                    rotated_transpose(soon, done)
                if now:
                    if next_:
                        pe.wait_ge(v_ready, next_.n + 1)
                    weigh_values(now)

            layers(pe, start, slot, mlp_slot)


def attention(nc, sems, X, Y, ident, ones_row, bank, B, MT, wq_in, bq_in, wk_in, bk_in, wv_in, bv_in,
              wo_in, bo_in):
    N = MT * P
    with ExitStack() as ctx:
        sb = lambda n, s, dt=F32: ctx.enter_context(nc.sbuf_tensor(f"att_{n}", s, dt))
        sem = lambda n: sems(f"att_{n}")
        ys_in = [sem(f"ys_in{i}") for i in range(2)]
        w = sb("w", [P, 4, P])
        bias = sb("bias", [P, 3])
        bo = sb("bo", [1, P])
        bo_all = sb("bo_all", [P, P])
        ys = sb("ys", [P, 2, MT, P])
        xT = sb("xT", [P, N])
        qkvT = sb("qkvT", [P, 2, 3, N])
        vo = sb("vo", [P, 2, MT, P + 1])
        th_half = sb("th_half", [P, 2, N])
        th_full = sb("th_full", [P, 2, N])
        mix = sb("mix", [P, N])
        theta = sb("theta", [P, 2, N])
        top = sb("top", [P, 2])
        bias_top = sb("bias_top", [P, 2])
        probs = sb("probs", [P, 2, N])
        probsT = sb("probsT", [P, 2, N])
        rsum = sb("rsum", [P, 2])
        o = sb("o", [P, 2, P])
        (w_in, bo_psum, bo_ready, xT_psum, xT_ready, proj_psum, proj_ready, vo_psum, vo_ready,
         ones_done, scores_ready, half_ready, full_ready, mix_ready, theta_ready, top_ready, bias_ready,
         probs_ready, pT_psum, pT_ready, out_psum, rsum_ready, o_ready, x_ready) = map(
            sem, """w_in bo_psum bo_ready xT_psum xT_ready proj_psum proj_ready vo_psum vo_ready
            ones_done scores_ready half_ready full_ready mix_ready theta_ready top_ready bias_ready
            probs_ready pT_psum pT_ready out_psum rsum_ready o_ready x_ready""".split())
        block = ctx.enter_context(nc.Block())

        PIECES = [[("x", 0), ("x", 1)], [("p", 0), ("p", 1)], [("p", 2)], [("p", 3)],
                  [("p", 4)], [("p", 5)], [("o", 0)], [("o", 1)]]

        def slots(engine, prepare, slot):
            def at(k, n, m, d):
                if isinstance(k, int):
                    k += d
                    return (k, k // MT, k % MT) if 0 <= k < B * MT else None
                return k + d, n + (m + d) // MT, (m + d) % MT

            def parity(n, par, m, d):
                return (par + (m + d) // MT) % 2

            def one(k, n, par, m):
                def tile(d):
                    found = at(k, n, m, d)
                    return found and Query(*found, parity(n, par, m, d))
                more = not isinstance(n, int) or 0 <= n < B - 1
                slot(tile, (n + 1, 1 - par, PIECES[m]) if more and 0 <= m < MT else None)

            for pieces in PIECES:
                for piece in pieces:
                    prepare(0, 0, piece)
            one(-1, 0, 0, -1)
            for n in range(2):
                for m in range(MT):
                    one(n * MT + m, n, n, m)
            with engine.Fori(1, B // 2 - 1) as b2:
                for par in range(2):
                    for m in range(MT):
                        n = b2 * 2 + par
                        one(n * MT + m, n, par, m)
            for n in range(B - 2, B):
                for m in range(MT):
                    one(n * MT + m, n, n % 2, m)
            for d in range(3):
                one(B * MT + d, B - 1, (B - 1) % 2, MT + d)

        @block.sync
        def _(sp):
            for i, t in enumerate((wq_in, wk_in, wv_in, wo_in)):
                sp.dma_start(w[:, i, :], t).then_inc(w_in, 16)
            for i, t in enumerate((bq_in, bk_in, bv_in)):
                sp.dma_start(bias[:, i:i + 1], t.rearrange("(p o) -> p o", o=1)).then_inc(w_in, 16)
            sp.dma_start(bo[:], bo_in.rearrange("(o p) -> o p", o=1)).then_inc(w_in, 16)
            for b in range(2):
                sp.dma_start(ys[:, b], Y[:, b * MT:(b + 1) * MT, :]).then_inc(ys_in[b], 16)
            with sp.Fori(0, B // 2 - 1) as b2:
                for b in range(2):
                    row = sp.snap((b2 * 2 + b + 2) * MT)
                    wait(sp, xT_psum, 4 * b2 + 2 * b + 2)
                    sp.dma_start(ys[:, b], Y[:, bass.ds(row, MT), :]).then_inc(ys_in[b], 16)

        @block.tensor
        def _(pe):
            wait(pe, w_in, 16 * 8)
            nc.tensor.matmul(bank(7, 0, P), ones_row[:], bo[:], start=True, stop=True).then_inc(bo_psum, 1)
            wait(pe, bo_ready, 1)
            wait(pe, ones_done, 1)

            def prepare(n, par, piece):
                kind, i = piece
                if kind == "x":
                    if i == 0:
                        wait(pe, ys_in[par], 8 * (n - par) + 16)
                        wait(pe, vo_ready, 2 * n)
                    else:
                        wait(pe, xT_ready, 2 * n + 1)
                    for m in range(4 * i, 4 * i + 4):
                        last = nc.tensor.transpose(bank(7, (m % 4) * P, (m % 4 + 1) * P), ys[:, par, m, :], ident[:])
                    last.then_inc(xT_psum, 1)
                elif kind == "p":
                    if i == 0:
                        wait(pe, xT_ready, 2 * n + 2)
                    else:
                        wait(pe, proj_ready, 6 * n + i)
                    nc.tensor.matmul(bank(7), w[:, i // 2, :], xT[:, (i % 2) * BANK:(i % 2 + 1) * BANK],
                                     start=True, stop=True).then_inc(proj_psum, 1)
                else:
                    if i == 0:
                        wait(pe, proj_ready, 6 * n + 6)
                    else:
                        wait(pe, vo_ready, 2 * n + 1)
                    for m in range(4 * i, 4 * i + 4):
                        last = nc.tensor.matmul(bank(7, (m % 4) * P, (m % 4 + 1) * P),
                                                qkvT[:, par, 2, m * P:(m + 1) * P], w[:, 3, :], start=True, stop=True)
                    last.then_inc(vo_psum, 1)

            def slot(tile, pieces):
                if t := tile(1):
                    if t.m == 0:
                        wait(pe, proj_ready, 6 * t.n + 4)
                    wait(pe, theta_ready, t.k - 1)
                    wait(pe, full_ready, t.k - 1)
                    for half in range(2):
                        last = nc.tensor.matmul(bank(2 * (t.m % 2) + half), qkvT[:, t.par, 0, t.m * P:(t.m + 1) * P],
                                                qkvT[:, t.par, 1, half * BANK:(half + 1) * BANK], start=True, stop=True)
                    last.then_inc(scores_ready, 1)
                if t := tile(-1):
                    wait(pe, probs_ready, t.k + 1)
                    for i in range(2):
                        wait(pe, pT_ready, 2 * t.k)
                        for c in range(4 * i, 4 * i + 4):
                            last = nc.tensor.transpose(bank(4 + i, (c % 4) * P, (c % 4 + 1) * P),
                                                       probs[:, t.m % 2, c * P:(c + 1) * P], ident[:])
                        last.then_inc(pT_psum, 1)
                if pieces:
                    prepare(pieces[0], pieces[1], pieces[2][0])
                if t := tile(-2):
                    wait(pe, pT_ready, 2 * t.k + 2)
                    wait(pe, o_ready, t.k)
                    if t.m == 0:
                        wait(pe, vo_ready, 2 * t.n + 2)
                    for c in range(MT):
                        last = nc.tensor.matmul(bank(6, 0, P + 1), probsT[:, t.m % 2, c * P:(c + 1) * P],
                                                vo[:, t.par, c, :], start=(c == 0), stop=(c == MT - 1))
                    last.then_inc(out_psum, 1)
                if pieces and len(pieces[2]) > 1:
                    prepare(pieces[0], pieces[1], pieces[2][1])

            slots(pe, prepare, slot)

        @block.scalar
        def _(act):
            def prepare(n, par, piece):
                kind, i = piece
                if kind == "x":
                    wait(act, xT_psum, 2 * n + i + 1)
                    wait(act, proj_psum, 6 * n)
                    nc.scalar.copy(xT[:, i * BANK:(i + 1) * BANK], bank(7)).then_inc(xT_ready, 1)
                elif kind == "o":
                    wait(act, vo_psum, 2 * n + i + 1)
                    nc.scalar.copy(vo[:, par, 4 * i:4 * i + 4, 0:P],
                                   bank(7).rearrange("p (m d) -> p m d", d=P)).then_inc(vo_ready, 1)

            def slot(tile, pieces):
                if t := tile(-1):
                    q = t.m % 2
                    wait(act, bias_ready, t.k + 1)
                    wait(act, pT_psum, 2 * (t.k - 1))
                    nc.scalar.activation(probs[:, q, :], theta[:, q, :], ACT.Exp, bias=bias_top[:, q:q + 1],
                                         scale=0.1).then_inc(probs_ready, 1)
                if t := tile(1):
                    s = wide(bank, 2 * (t.m % 2))
                    wait(act, scores_ready, t.k + 1)
                    wait(act, mix_ready, t.k - 1)
                    nc.scalar.activation(th_half[:, t.m % 2, :], s, ACT.Tanh, scale=0.5).then_inc(half_ready, 1)
                    nc.scalar.activation(th_full[:, t.m % 2, :], s, ACT.Tanh).then_inc(full_ready, 1)
                if t := tile(-1):
                    wait(act, out_psum, t.k - 1)
                    for i in range(2):
                        wait(act, pT_psum, 2 * t.k + i + 1)
                        nc.scalar.copy(probsT[:, t.m % 2, i * BANK:(i + 1) * BANK], bank(4 + i)).then_inc(pT_ready, 1)
                if pieces:
                    for piece in pieces[2]:
                        prepare(pieces[0], pieces[1], piece)

            slots(act, prepare, slot)

        @block.vector
        def _(dve):
            nc.vector.memset(vo[:, :, :, P:P + 1], 1.0).then_inc(ones_done, 1)
            wait(dve, bo_psum, 1)
            nc.vector.tensor_copy(bo_all[:], bank(7, 0, P)).then_inc(bo_ready, 1)

            def prepare(n, par, piece):
                kind, i = piece
                if kind == "p":
                    wait(dve, proj_psum, 6 * n + i + 1)
                    nc.vector.tensor_scalar(qkvT[:, par, i // 2, (i % 2) * BANK:(i % 2 + 1) * BANK], bank(7),
                                            bias[:, i // 2:i // 2 + 1], None, ALU.add).then_inc(proj_ready, 1)

            def slot(tile, pieces):
                if t := tile(-3):
                    q = t.m % 2
                    acc = bank(6, 0, P + 1)
                    wait(dve, out_psum, t.k + 1)
                    nc.vector.reciprocal(rsum[:, q:q + 1], acc[:, P:P + 1]).then_inc(rsum_ready, 1)
                    wait(dve, rsum_ready, t.k + 1)
                    nc.vector.scalar_tensor_tensor(out=o[:, q, :], in0=acc[:, 0:P], scalar=rsum[:, q:q + 1],
                                                   in1=bo_all[:], op0=ALU.mult, op1=ALU.add).then_inc(o_ready, 1)
                if t := tile(0):
                    q = t.m % 2
                    wait(dve, full_ready, t.k + 1)
                    wait(dve, theta_ready, t.k)
                    nc.vector.scalar_tensor_tensor(out=mix[:], in0=th_full[:, q, :], scalar=1.5,
                                                   in1=th_half[:, q, :], op0=ALU.mult, op1=ALU.add).then_inc(mix_ready, 1)
                if u := tile(-3):
                    wait(dve, o_ready, u.k + 1)
                    xs = X[:, bass.ds(u.k, 1), :].rearrange("p o d -> p (o d)")
                    nc.vector.tensor_tensor(xs, xs, o[:, u.m % 2, :], ALU.add).then_inc(x_ready, 1)
                if t := tile(0):
                    wait(dve, mix_ready, t.k + 1)
                    wait(dve, probs_ready, t.k - 1)
                    nc.vector.scalar_tensor_tensor(out=theta[:, q, :], in0=wide(bank, 2 * q), scalar=0.0,
                                                   in1=mix[:], op0=ALU.max, op1=ALU.add).then_inc(theta_ready, 1)
                    wait(dve, theta_ready, t.k + 1)
                    nc.vector.tensor_reduce(top[:, q:q + 1], theta[:, q, :], AX_X, ALU.max).then_inc(top_ready, 1)
                    wait(dve, top_ready, t.k + 1)
                    nc.vector.tensor_scalar(bias_top[:, q:q + 1], top[:, q:q + 1], -0.1, None,
                                            ALU.mult).then_inc(bias_ready, 1)
                if pieces:
                    for piece in pieces[2]:
                        prepare(pieces[0], pieces[1], piece)

            slots(dve, prepare, slot)
            wait(dve, x_ready, B * MT)


def wide(bank, i):
    return bank(i, 0, 2 * BANK)


_INS = ['L0_attn_x', 'L0_attn_Wq', 'L0_attn_bq', 'L0_attn_Wk', 'L0_attn_bk', 'L0_attn_Wv', 'L0_attn_bv',
        'L0_attn_Wo', 'L0_attn_bo', 'L0_ffn_wqkv', 'L0_ffn_q_scale', 'L0_ffn_k_scale', 'L0_ffn_wo',
        'L0_ffn_ln_g', 'L0_ffn_ln_b', 'L0_ffn_w1', 'L0_ffn_b1', 'L0_ffn_w2', 'L0_ffn_b2']
_TRANSPOSED = ('L0_attn_Wq', 'L0_attn_Wk', 'L0_attn_Wv', 'L0_attn_Wo')


def kernel(**inputs):
    import concourse.bacc as bacc
    from concourse.bass_utils import run_bass_kernel_spmd

    nc = bacc.Bacc("TRN2", target_bir_lowering=False, num_devices=1)
    arrays, args = {}, []

    def declare(name, a):
        arrays[name] = a
        args.append(nc.dram_tensor(name, a.shape, mybir.dt.from_np(a.dtype), kind="ExternalInput").ap())

    for name in _INS:
        a = np.asarray(inputs[name])
        declare(f"in_{name}", np.ascontiguousarray(a.T if name in _TRANSPOSED else a))
    shape = inputs['L0_attn_x'].shape
    declare("rotary", rotary_tables(shape[1]))
    declare("masks", window_masks())
    declare("identity", np.eye(P, dtype=np.float32))
    args.append(nc.dram_tensor("out_0", shape, F32, kind="ExternalOutput").ap())
    macaron(nc, *args)
    r = run_bass_kernel_spmd(nc, [arrays], core_ids=[0])
    return r.results[0]["out_0"]
```
